# Optimizing a Trainium2 kernel written in Bass

```python
import numpy as np
import jax
import jax.numpy as jnp

def _softmax(x, axis=-1):
    return jax.nn.softmax(x, axis=axis)
def _gelu(x):
    return jax.nn.gelu(x, approximate=True)
def _silu(x):
    return jax.nn.silu(x)
def _sigmoid(x):
    return jax.nn.sigmoid(x)
def _layernorm(x, axis=-1, eps=1e-5):
    m = jnp.mean(x, axis=axis, keepdims=True)
    v = jnp.var(x, axis=axis, keepdims=True)
    return (x - m) / jnp.sqrt(v + eps)
def _scatter_add(tgt, idx, src, axis=0):
    return tgt.at[idx].add(src)
def _segment_sum(src, seg, n):
    return jax.ops.segment_sum(src, seg, n)

kernel_name = 'mk_conv_seq_d1_conv_nchw16_5d5294'

def setup_inputs(seed: int = 0):
    np.random.seed(seed)
    _w = jnp.asarray
    def _rec_inputs():
        import jax
        import jax.numpy as jnp
        _gk = jax.random.key(seed)
        x = -0.0001266 + 0.9999 * jax.random.normal(jax.random.fold_in(_gk, 1), (16, 16, 197, 768), jnp.float32)
        return x
    x = _rec_inputs()
    def _L0_conv_setup():
        import math
        import jax
        import jax.numpy as jnp
        import numpy as np
        from jax import lax
        HEADS = 4
        TOPK = 8

        def _gelu(x):
            return jax.nn.gelu(x, approximate=False)

        def _ln(x, g, b, eps=1e-05):
            m = x.mean(-1, keepdims=True)
            v = ((x - m) ** 2).mean(-1, keepdims=True)
            return (x - m) * lax.rsqrt(v + eps) * g + b
        key = jax.random.key(seed)
        ks = jax.random.split(key, 16)
        B, T, N, C, A = (16, 16, 196, 768, 192)

        def w(k, shape, s=0.02):
            return jax.random.normal(k, shape, jnp.float32) * s
        return dict(x=w(ks[0], (B, T, N + 1, C), 1.0), down_w=w(ks[1], (A, C)), down_b=jnp.zeros((A,), jnp.float32), ldw_w=w(ks[2], (A, 1, 3, 3), 0.1), lpw_w=w(ks[3], (A, A), 0.05), lnorm_g=jnp.ones((A,), jnp.float32), lnorm_b=jnp.zeros((A,), jnp.float32), tdw_w=w(ks[4], (A, 1, 3), 0.1), tpw_w=w(ks[5], (A, A), 0.05), tmlp_w1=w(ks[6], (2 * A, A), 0.05), tmlp_b1=jnp.zeros((2 * A,), jnp.float32), tmlp_w2=w(ks[7], (A, 2 * A), 0.05), tmlp_b2=jnp.zeros((A,), jnp.float32), tnorm_g=jnp.ones((A,), jnp.float32), tnorm_b=jnp.zeros((A,), jnp.float32), attn_in_w=w(ks[8], (3 * A, A), 0.05), attn_in_b=jnp.zeros((3 * A,), jnp.float32), attn_out_w=w(ks[9], (A, A), 0.05), attn_out_b=jnp.zeros((A,), jnp.float32), aproj_w=w(ks[10], (A, A), 0.05), aproj_b=jnp.zeros((A,), jnp.float32), anorm_g=jnp.ones((A,), jnp.float32), anorm_b=jnp.zeros((A,), jnp.float32), gate_w1=w(ks[11], (A, 2 * A), 0.05), gate_b1=jnp.zeros((A,), jnp.float32), gate_w2=w(ks[12], (3 * A, A), 0.05), gate_b2=jnp.zeros((3 * A,), jnp.float32), up_w=w(ks[13], (C, A), 0.02), up_b=jnp.zeros((C,), jnp.float32), cls_w=w(ks[14], (C, A), 0.02), cls_b=jnp.zeros((C,), jnp.float32))
    _L0_conv_all = _L0_conv_setup()
    _L0_conv_in = {k: v for k, v in _L0_conv_all.items() if k in ('down_w', 'down_b', 'ldw_w', 'lpw_w', 'lnorm_g', 'lnorm_b', 'tdw_w', 'tpw_w', 'tmlp_w1', 'tmlp_b1', 'tmlp_w2', 'tmlp_b2', 'tnorm_g', 'tnorm_b', 'attn_in_w', 'attn_in_b', 'attn_out_w', 'attn_out_b', 'aproj_w', 'aproj_b', 'anorm_g', 'anorm_b', 'gate_w1', 'gate_b1', 'gate_w2', 'gate_b2', 'up_w', 'up_b', 'cls_w', 'cls_b', )}
    del _L0_conv_all

    return {
        "x": x,
        "L0_conv_down_w": _L0_conv_in["down_w"],
        "L0_conv_down_b": _L0_conv_in["down_b"],
        "L0_conv_ldw_w": _L0_conv_in["ldw_w"],
        "L0_conv_lpw_w": _L0_conv_in["lpw_w"],
        "L0_conv_lnorm_g": _L0_conv_in["lnorm_g"],
        "L0_conv_lnorm_b": _L0_conv_in["lnorm_b"],
        "L0_conv_tdw_w": _L0_conv_in["tdw_w"],
        "L0_conv_tpw_w": _L0_conv_in["tpw_w"],
        "L0_conv_tmlp_w1": _L0_conv_in["tmlp_w1"],
        "L0_conv_tmlp_b1": _L0_conv_in["tmlp_b1"],
        "L0_conv_tmlp_w2": _L0_conv_in["tmlp_w2"],
        "L0_conv_tmlp_b2": _L0_conv_in["tmlp_b2"],
        "L0_conv_tnorm_g": _L0_conv_in["tnorm_g"],
        "L0_conv_tnorm_b": _L0_conv_in["tnorm_b"],
        "L0_conv_attn_in_w": _L0_conv_in["attn_in_w"],
        "L0_conv_attn_in_b": _L0_conv_in["attn_in_b"],
        "L0_conv_attn_out_w": _L0_conv_in["attn_out_w"],
        "L0_conv_attn_out_b": _L0_conv_in["attn_out_b"],
        "L0_conv_aproj_w": _L0_conv_in["aproj_w"],
        "L0_conv_aproj_b": _L0_conv_in["aproj_b"],
        "L0_conv_anorm_g": _L0_conv_in["anorm_g"],
        "L0_conv_anorm_b": _L0_conv_in["anorm_b"],
        "L0_conv_gate_w1": _L0_conv_in["gate_w1"],
        "L0_conv_gate_b1": _L0_conv_in["gate_b1"],
        "L0_conv_gate_w2": _L0_conv_in["gate_w2"],
        "L0_conv_gate_b2": _L0_conv_in["gate_b2"],
        "L0_conv_up_w": _L0_conv_in["up_w"],
        "L0_conv_up_b": _L0_conv_in["up_b"],
        "L0_conv_cls_w": _L0_conv_in["cls_w"],
        "L0_conv_cls_b": _L0_conv_in["cls_b"],
    }

def reference(x, L0_conv_down_w, L0_conv_down_b, L0_conv_ldw_w, L0_conv_lpw_w, L0_conv_lnorm_g, L0_conv_lnorm_b, L0_conv_tdw_w, L0_conv_tpw_w, L0_conv_tmlp_w1, L0_conv_tmlp_b1, L0_conv_tmlp_w2, L0_conv_tmlp_b2, L0_conv_tnorm_g, L0_conv_tnorm_b, L0_conv_attn_in_w, L0_conv_attn_in_b, L0_conv_attn_out_w, L0_conv_attn_out_b, L0_conv_aproj_w, L0_conv_aproj_b, L0_conv_anorm_g, L0_conv_anorm_b, L0_conv_gate_w1, L0_conv_gate_b1, L0_conv_gate_w2, L0_conv_gate_b2, L0_conv_up_w, L0_conv_up_b, L0_conv_cls_w, L0_conv_cls_b):
    import jax
    import jax.numpy as jnp
    def _L0_conv_ref(x, down_w, down_b, ldw_w, lpw_w, lnorm_g, lnorm_b, tdw_w, tpw_w, tmlp_w1, tmlp_b1, tmlp_w2, tmlp_b2, tnorm_g, tnorm_b, attn_in_w, attn_in_b, attn_out_w, attn_out_b, aproj_w, aproj_b, anorm_g, anorm_b, gate_w1, gate_b1, gate_w2, gate_b2, up_w, up_b, cls_w, cls_b):
        import math
        import jax
        import jax.numpy as jnp
        import numpy as np
        from jax import lax
        HEADS = 4
        TOPK = 8

        def _gelu(x):
            return jax.nn.gelu(x, approximate=False)

        def _ln(x, g, b, eps=1e-05):
            m = x.mean(-1, keepdims=True)
            v = ((x - m) ** 2).mean(-1, keepdims=True)
            return (x - m) * lax.rsqrt(v + eps) * g + b
        cls_tok = x[:, :, :1, :]
        patch = x[:, :, 1:, :]
        b, t, n, _ = patch.shape
        hw = int(math.isqrt(n))
        a = down_w.shape[0]
        ph = jnp.einsum('btnc,ac->btna', patch, down_w) + down_b
        delta = jnp.concatenate([jnp.zeros_like(ph[:, :1]), ph[:, 1:] - ph[:, :-1]], axis=1)
        loc = ph.reshape(b * t, hw, hw, a).transpose(0, 3, 1, 2)
        loc = lax.conv_general_dilated(loc, ldw_w, (1, 1), 'SAME', feature_group_count=a, dimension_numbers=('NCHW', 'OIHW', 'NCHW'))
        loc = _gelu(loc)
        loc = jnp.einsum('bchw,dc->bdhw', loc, lpw_w)
        loc = loc.transpose(0, 2, 3, 1).reshape(b, t, n, a)
        local = _ln(loc, lnorm_g, lnorm_b)
        tr = delta.transpose(0, 2, 3, 1).reshape(b * n, a, t)
        tr = lax.conv_general_dilated(tr, tdw_w, (1,), 'SAME', feature_group_count=a, dimension_numbers=('NCH', 'OIH', 'NCH'))
        tr = _gelu(tr)
        tr = jnp.einsum('nct,dc->ndt', tr, tpw_w)
        tr = tr.reshape(b, n, a, t).transpose(0, 3, 1, 2)
        h1 = _gelu(jnp.einsum('btna,ha->btnh', tr, tmlp_w1) + tmlp_b1)
        tr = jnp.einsum('btnh,ah->btna', h1, tmlp_w2) + tmlp_b2
        transition = _ln(tr, tnorm_g, tnorm_b)
        kk = min(TOPK, n)
        sal = jnp.abs(delta).mean(-1)
        _, idx = lax.top_k(sal, kk)
        bi = jnp.arange(b)[:, None, None]
        ti = jnp.arange(t)[None, :, None]
        anchor = (ph + delta)[bi, ti, idx]
        tok = anchor.transpose(0, 2, 1, 3).reshape(b * kk, t, a)
        qkv = tok @ attn_in_w.T + attn_in_b
        q, k_, v = jnp.split(qkv, 3, axis=-1)
        dh = a // HEADS

        def heads(z):
            return z.reshape(b * kk, t, HEADS, dh).transpose(0, 2, 1, 3)
        q, k_, v = (heads(q), heads(k_), heads(v))
        att = jax.nn.softmax(jnp.einsum('bhqd,bhkd->bhqk', q, k_) / math.sqrt(dh), axis=-1)
        out = jnp.einsum('bhqk,bhkd->bhqd', att, v).transpose(0, 2, 1, 3).reshape(b * kk, t, a)
        out = out @ attn_out_w.T + attn_out_b
        out = out @ aproj_w.T + aproj_b
        anchor_tok = out.reshape(b, kk, t, a).transpose(0, 2, 1, 3)
        anchor_map = jnp.zeros_like(ph).at[bi, ti, idx].add(anchor_tok)
        anchor_map = _ln(anchor_map, anorm_g, anorm_b)
        dp = jnp.abs(delta).mean((1, 2))
        ap = anchor_tok.mean((1, 2))
        g = jnp.concatenate([dp, ap], axis=-1)
        g = _gelu(g @ gate_w1.T + gate_b1) @ gate_w2.T + gate_b2
        gw = jax.nn.softmax(g.reshape(b, 3, a), axis=1)[:, :, None, None, :]
        fused = gw[:, 0] * local + gw[:, 1] * transition + gw[:, 2] * anchor_map
        patch_out = patch + fused @ up_w.T + up_b
        cls_out = cls_tok + fused.mean(2, keepdims=True) @ cls_w.T + cls_b
        return jnp.concatenate([cls_out, patch_out], axis=2)

    def _gn(v, G=8, eps=1e-5):
        B_, C_, H_, W_ = v.shape
        g = v.reshape(B_, G, C_ // G, H_, W_)
        m = jnp.mean(g, axis=(2, 3, 4), keepdims=True)
        s = jnp.var(g, axis=(2, 3, 4), keepdims=True)
        return ((g - m) / jnp.sqrt(s + eps)).reshape(v.shape)

    def _ln_c(v, eps=1e-6):
        m = jnp.mean(v, axis=1, keepdims=True)
        s = jnp.var(v, axis=1, keepdims=True)
        return (v - m) / jnp.sqrt(s + eps)

    def _ln_t(v, eps=1e-5):
        m = jnp.mean(v, axis=-1, keepdims=True)
        s = jnp.var(v, axis=-1, keepdims=True)
        return (v - m) / jnp.sqrt(s + eps)

    def _to_tokens(v):
        B_, C_, H_, W_ = v.shape
        return v.reshape(B_, C_, H_ * W_).transpose(0, 2, 1)
    def _from_tokens(t, like):
        B_, C_, H_, W_ = like.shape
        return t.transpose(0, 2, 1).reshape(B_, C_, H_, W_)

    x = _L0_conv_ref(x, L0_conv_down_w, L0_conv_down_b, L0_conv_ldw_w, L0_conv_lpw_w, L0_conv_lnorm_g, L0_conv_lnorm_b, L0_conv_tdw_w, L0_conv_tpw_w, L0_conv_tmlp_w1, L0_conv_tmlp_b1, L0_conv_tmlp_w2, L0_conv_tmlp_b2, L0_conv_tnorm_g, L0_conv_tnorm_b, L0_conv_attn_in_w, L0_conv_attn_in_b, L0_conv_attn_out_w, L0_conv_attn_out_b, L0_conv_aproj_w, L0_conv_aproj_b, L0_conv_anorm_g, L0_conv_anorm_b, L0_conv_gate_w1, L0_conv_gate_b1, L0_conv_gate_w2, L0_conv_gate_b2, L0_conv_up_w, L0_conv_up_b, L0_conv_cls_w, L0_conv_cls_b)
    return x


_drawn_inputs = setup_inputs


def setup_inputs(seed=0):
    import zlib

    import numpy as np

    out = dict(_drawn_inputs(seed))
    spreads = {'L0_conv_down_b': (0.0, 0.445),
     'L0_conv_lnorm_g': (1.0, 0.6),
     'L0_conv_lnorm_b': (0.0, 0.8),
     'L0_conv_tmlp_b1': (0.0, 0.8),
     'L0_conv_tmlp_b2': (0.0, 0.795),
     'L0_conv_tnorm_g': (1.0, 0.6),
     'L0_conv_tnorm_b': (0.0, 0.8),
     'L0_conv_attn_in_b': (0.0, 0.8),
     'L0_conv_attn_out_b': (0.0, 0.8),
     'L0_conv_aproj_b': (0.0, 0.731),
     'L0_conv_anorm_g': (1.0, 0.6),
     'L0_conv_anorm_b': (0.0, 0.8),
     'L0_conv_gate_b1': (0.0, 2.0),
     'L0_conv_gate_b2': (0.0, 0.71),
     'L0_conv_up_b': (0.0, 0.1),
     'L0_conv_cls_b': (0.0, 0.8)}
    factors = {'L0_conv_tdw_w': 4.527,
     'L0_conv_tpw_w': 4.406,
     'L0_conv_tmlp_w1': 4.426,
     'L0_conv_attn_in_w': 3.529,
     'L0_conv_attn_out_w': 3.438,
     'L0_conv_aproj_w': 3.083,
     'L0_conv_gate_w1': 3.012,
     'L0_conv_cls_w': 8.0}
    for name, (base, spread) in spreads.items():
        noise = np.random.default_rng([zlib.crc32(name.encode()), seed]).standard_normal(out[name].shape)
        drawn = base * np.exp(spread * noise) if base else spread * noise
        out[name] = jnp.asarray(drawn.astype(out[name].dtype))
    for name, factor in factors.items():
        out[name] = (out[name] * factor).astype(out[name].dtype)
    return out
```

```python
from contextlib import ExitStack

import concourse.bass as bass
from concourse import mybir

F32 = mybir.dt.float32
U32 = mybir.dt.uint32
ACT = mybir.ActivationFunctionType
ALU = mybir.AluOpType
AX = mybir.AxisListType

B, T, SIDE, C, A = 16, 16, 14, 768, 192
HW = SIDE * SIDE
PT = 2 * HW
HA = A // 2
KC = C // 128
PAIRS = T // 2
NPAIR = B * PAIRS
HID = 2 * A
KH = HID // 128
TOPK, HEADS = 8, 4
DH = A // HEADS
NANC = T * TOPK
EPS = 1e-5
PITCH = SIDE + 1
FP = PITCH * PITCH
GUARD = PITCH + 1
ROWS = 2 * SIDE + 1
SPAN = ROWS * PITCH

V96 = {}
_at = 0
for _name, _n in (("down_b", 2), ("gain", 6), ("beta", 6), ("mlp_b2", 2), ("out_b", 2), ("proj_b", 2),
                  ("gate_b1", 2), ("gate_b2", 6), ("ldw", 18), ("tdw", 6)):
    V96[_name] = (_at, _n)
    _at += _n
NV96 = _at
W96 = {}
_at = 0
for _name, _n in (("lpw", 2 * A), ("up", 2 * C), ("attn_in", 2 * 3 * A), ("aproj", 2 * A),
                  ("gate1", 4 * A), ("gate2", 2 * 3 * A)):
    W96[_name] = (_at, _n)
    _at += _n
NW96 = _at
NSETUP = 2 * A + 2 * HID

CHAIN = {
    "pe": ["qk", "v", "scores", "turned", "mixed", "out", "anchor", "mean_gate1", "var", "gate2"],
    "act": ["v", "exp", "square", "gelu", "gate_exp", "rsqrt", "rsqrt_sq"],
    "dve": ["dp", "dp_scaled", "tok", "q", "k", "masked", "max", "shifted", "sum", "recip", "prob",
            "turned", "mixed", "out", "anchor", "ap", "ap_scaled", "centred", "gate1", "gate2",
            "gmax1", "gmax2", "gshift", "gsum1", "gsum2", "grecip", "gates", "gains", "betas",
            "const1", "const2", "newton1", "newton2", "newton3", "znorm", "z"],
}


def after(engine, clip, step):
    steps = CHAIN[engine]
    return clip * len(steps) + (steps.index(step) + 1)


def build(nc, xp, xcls, wdown, w96, wsetup, wcls, w2, aout, v96, v48, v128, consts, out, outcls):
    ds = bass.ds
    with ExitStack() as ctx:
        def sb(name, shape, dt=F32):
            return ctx.enter_context(nc.sbuf_tensor(name, shape, dt))

        def sem(name):
            return ctx.enter_context(nc.semaphore(name))

        WD = sb("WD", [128, KC, A])
        W = sb("W", [HA, NW96])
        W1P = sb("W1P", [HA, 2, HID])
        W2 = sb("W2", [128, KH, A])
        AOUT = sb("AOUT", [DH, HEADS, A])
        VA = sb("VA", [HA, NV96])
        VH = sb("VH", [DH, 3, HEADS])
        VP = sb("VP", [128, KH + 2 * KC])
        CST = sb("CST", [128, 2, 128])
        ONES = sb("ONES", [HA, 128])
        EPSC = sb("EPSC", [HA, 1])
        WM = sb("WM", [128, 8])

        def wt(name, n):
            a, m = W96[name]
            return W[:, a:a + m].rearrange("p (k n) -> p k n", n=n)

        def vec(name):
            a, m = V96[name]
            return VA[:, a:a + m]

        LPW, UP, AIN = wt("lpw", A), wt("up", C), wt("attn_in", 3 * A)
        APR, GW1, GW2 = wt("aproj", A), wt("gate1", A), wt("gate2", 3 * A)
        LDW = vec("ldw").rearrange("p (h k) -> p h k", k=9)
        TDW = vec("tdw").rearrange("p (h k) -> p h k", k=3)
        IDENT, MASK = CST[:, 0, :], CST[:, 1, :]

        XA = sb("XA", [128, KC, PT])
        XC = sb("XC", [128, KC, PT])
        PH = sb("PH", [HA, 2, GUARD + 4 * FP + 2])
        DL = sb("DL", [HA, 2, T + 2, HW])
        NRM = sb("NRM", [HA, 4, PAIRS, PT])
        CV = sb("CV", [HA, 2, 2 * FP])
        TV = sb("TV", [HA, 2, PT])
        GL = sb("GL", [HA, 2, PT])
        H1 = sb("H1", [128, KH, PT])
        AD = sb("AD", [HA, 2, PT])
        ADS = sb("ADS", [HA, PT])
        SQ = sb("SQ", [HA, 2, PT])
        SQS = sb("SQS", [HA, 2, PT])
        RY = sb("RY", [HA, 2, PT])
        RT = sb("RT", [HA, 2, PT])
        FT = sb("FT", [HA, 2, PT])
        FU = sb("FU", [HA, 2, 2, PT])
        FS = sb("FS", [HA, 2, B * T])
        MX = sb("MX", [1, 2, TOPK])
        IDN = sb("IDN", [1, 2 * TOPK], U32)
        IDX = sb("IDX", [1, 2 * PAIRS, 2 * TOPK], U32)
        DPS = sb("DPS", [HA, 2, 2, PAIRS])
        G = sb("G", [HA, 2, 4, NANC])
        TOK = sb("TOK", [HA, 2, NANC])
        QH = sb("QH", [DH, HEADS, NANC])
        KHD = sb("KHD", [DH, HEADS, NANC])
        VV = sb("VV", [NANC, A])
        S = sb("S", [NANC, HEADS, NANC])
        ST = sb("ST", [NANC, HEADS, NANC])
        SM = sb("SM", [NANC, 3, HEADS])
        OH = sb("OH", [DH, HEADS, NANC])
        A1 = sb("A1", [HA, 2, NANC])
        A2 = sb("A2", [HA, 2, NANC])
        XCN = sb("XCN", [HA, 2, NANC])
        ASQ = sb("ASQ", [HA, 2, NANC])
        AY = sb("AY", [HA, NANC])
        AT = sb("AT", [HA, NANC])
        Z = sb("Z", [HA, 2, NANC])
        GIN = sb("GIN", [HA, 4])
        GH = sb("GH", [HA, 2])
        GT = sb("GT", [HA, 6])
        GM = sb("GM", [HA, 2])
        GG = sb("GG", [HA, 6])
        GB = sb("GB", [HA, 6])
        GC = sb("GC", [HA, 2])

        PS = ctx.enter_context(nc.psum_tensor("PS", [128, 8, 512], F32))

        wts_loaded = sem("wts_loaded")
        consts_set = sem("consts_set")
        holds = sem("holds")
        setup_pe = sem("setup_pe")
        setup_dve = sem("setup_dve")
        setup_act = sem("setup_act")
        xa_loaded = [sem(f"xa_loaded{h}") for h in range(2)]
        xc_loaded = [sem(f"xc_loaded{h}") for h in range(2)]
        stored = [sem(f"stored{h}") for h in range(2)]
        xa_used = sem("xa_used")
        ph_ready = sem("ph_ready")
        delta_ready = sem("delta_ready")
        abs_ready = sem("abs_ready")
        abs_summed = sem("abs_summed")
        sal_ready = sem("sal_ready")
        topk_step = sem("topk_step")
        gathered = sem("gathered")
        conv_taps = sem("conv_taps")
        conv_gelu = sem("conv_gelu")
        tconv_taps = sem("tconv_taps")
        tconv_gelu = sem("tconv_gelu")
        lpw_done = sem("lpw_done")
        local_out = sem("local_out")
        sq_ready = sem("sq_ready")
        sq_summed = sem("sq_summed")
        w1_done = sem("w1_done")
        h_ready = sem("h_ready")
        w2_done = sem("w2_done")
        trans_out = sem("trans_out")
        stats_done = sem("stats_done")
        rs_first = sem("rs_first")
        rs_square = sem("rs_square")
        newton_a = sem("newton_a")
        newton_b = sem("newton_b")
        newton_c = sem("newton_c")
        normed = sem("normed")
        weighted = sem("weighted")
        fused = sem("fused")
        scattered = sem("scattered")
        up_done = sem("up_done")
        resid = sem("resid")
        chain_pe = sem("chain_pe")
        chain_act = sem("chain_act")
        chain_dve = sem("chain_dve")
        cls_loaded = sem("cls_loaded")
        cls_mean = sem("cls_mean")
        cls_mm = sem("cls_mm")
        cls_out = sem("cls_out")
        cls_stored = sem("cls_stored")

        block = ctx.enter_context(nc.Block())

        WEIGHT_LOADS = 10

        def hold(eng, semaphore, value):
            eng.wait_ge(semaphore, value)
            eng.sem_inc(holds, 1)

        HK = KC // 2

        def halves(bank, n=PT, p=HA):
            return PS[0:p, bank:bank + 2, 0:n]

        def ph_base(slot):
            return GUARD + slot * (2 * FP)

        def window(tile, half, start, frames=2):
            v = tile[:, half, ds(start, frames * FP)]
            return v.rearrange("p (f r c) -> p f r c", r=PITCH, c=PITCH)[:, :, 0:SIDE, 0:SIDE]

        def frame2(tile, start):
            v = tile[:, :, ds(start, FP)]
            return v.rearrange("p h (r c) -> p h r c", c=PITCH)[:, :, 0:SIDE, 0:SIDE]

        def rows(tile, half, start):
            v = tile[:, half, ds(start, SPAN)]
            return v.rearrange("p (r c) -> p r c", c=PITCH)[:, :, 0:SIDE]

        @block.sync
        def _(sp):
            for h in range(2):
                sp.sem_inc(stored[h], 16)
            for dst, src in ((WD[:], wdown), (W[:], w96), (XC[0:HA].rearrange("p k n -> p (k n)")[:, 0:NSETUP], wsetup),
                             (W2[:], w2), (AOUT[:], aout), (VA[:], v96), (VH[:], v48), (VP[:], v128),
                             (CST[:], consts)):
                sp.dma_start(dst, src).then_inc(wts_loaded, 16)

            def load_xa(s):
                for h in range(2):
                    sp.wait_ge(xa_used, 2 * s + (h + 1))
                    sp.dma_start(XA[:, HK * h:HK * h + HK, :], xp[s, :, HK * h:HK * h + HK, :]).then_inc(xa_loaded[h], 16)

            def load_xc(k):
                for h in range(2):
                    sp.wait_ge(stored[h], 16 * k + 16)
                    sp.dma_start(XC[:, HK * h:HK * h + HK, :], xp[k, :, HK * h:HK * h + HK, :]).then_inc(xc_loaded[h], 16)

            def store(k):
                for h in range(2):
                    sp.wait_ge(resid, KC * k + (HK * (h + 1) + 2))
                    sp.dma_start(out[k, :, HK * h:HK * h + HK, :], XC[:, HK * h:HK * h + HK, :]).then_inc(stored[h], 16)

            AHEAD = PAIRS + 2
            for s in range(AHEAD):
                load_xa(s)
                if s == 1:
                    sp.wait_ge(setup_pe, 2)
            with sp.Fori(0, NPAIR - AHEAD) as k:
                load_xc(k)
                load_xa(k + AHEAD)
                store(k)
            with sp.Fori(NPAIR - AHEAD, NPAIR) as k:
                load_xc(k)
                store(k)
            sp.wait_ge(xa_used, 2 * NPAIR + 2)
            sp.dma_start(XA[:].rearrange("p k n -> p (k n)")[:, 0:KC * B * T], xcls).then_inc(cls_loaded, 16)
            for h in range(2):
                sp.wait_ge(stored[h], 16 * NPAIR + 16)
            sp.dma_start(XC[0:HA].rearrange("p k n -> p (k n)")[:, 0:2 * C], wcls).then_inc(cls_loaded, 16)
            sp.wait_ge(cls_out, KC)
            sp.dma_start(outcls, XA[:].rearrange("p k n -> p (k n)")[:, 0:KC * B * T]).then_inc(cls_stored, 16)
            sp.wait_ge(cls_stored, 16)

        @block.tensor
        def _(pe):
            setup = XC[0:HA].rearrange("p k n -> p (k n)")
            TPW = setup[:, 0:2 * A].rearrange("p (h c) -> p h c", h=2)
            W1T = setup[:, 2 * A:NSETUP].rearrange("p (h n) -> p h n", h=2)
            pe.wait_ge(wts_loaded, 16 * (WEIGHT_LOADS - 1))
            pe.wait_ge(consts_set, 4)
            for m in range(2):
                for h in range(2):
                    mm = nc.tensor.matmul(PS[0:HA, m, 0:HID], TPW[:, h, HA * m:HA * m + HA], W1T[:, h, :],
                                          start=(h == 0), stop=(h == 1))
                mm.then_inc(setup_pe, 1)
            b2 = vec("mlp_b2")
            for h in range(2):
                mm = nc.tensor.matmul(PS[0:HA, 2, 0:1], ONES[:, 0:HA], b2[:, h:h + 1], start=(h == 0), stop=(h == 1))
            mm.then_inc(setup_pe, 1)
            pe.sem_inc(xa_used, 2)
            for done in (w1_done, w2_done, stats_done):
                pe.sem_inc(done, 1)
            pe.wait_ge(setup_act, 1)
            pe.wait_ge(setup_dve, 7)

            def down(s):
                pe.wait_ge(h_ready, KH * s)
                for k in range(KC):
                    if k % HK == 0:
                        pe.wait_ge(xa_loaded[k // HK], 16 * s + 16)
                    for m in range(2):
                        mm = nc.tensor.matmul(PS[0:HA, m, 0:PT], WD[:, k, HA * m:HA * m + HA], XA[:, k, :],
                                              start=(k == 0), stop=(k == KC - 1))
                    if k % HK == HK - 1:
                        mm.then_inc(xa_used, 1)

            def local(s):
                pe.wait_ge(conv_gelu, 2 * s + 2)
                pe.wait_ge(trans_out, 2 * s + 1)
                for m in range(2):
                    for h in range(2):
                        mm = nc.tensor.matmul(PS[0:HA, 2 + m, 0:PT], LPW[:, h, HA * m:HA * m + HA], GL[:, h, :],
                                              start=(h == 0), stop=(h == 1))
                mm.then_inc(lpw_done, 1)

            def salience(s):
                pe.wait_ge(abs_summed, s + 1)
                pe.wait_ge(newton_a, s)
                nc.tensor.matmul(PS[0:1, 7, 0:PT], ONES[:, 0:1], ADS[:], start=True, stop=True).then_inc(sal_ready, 1)

            def hidden(s, with_a):
                pe.wait_ge(tconv_gelu, s + 1)
                if with_a:
                    pe.wait_ge(ph_ready, 2 * s + 4)
                pe.wait_ge(newton_a, s + 1)
                for m in range(KH):
                    for h in range(2):
                        mm = nc.tensor.matmul(PS[:, (0, 1, 6)[m], 0:PT], W1P[:, h, 128 * m:128 * m + 128], TV[:, h, :],
                                              start=(h == 0), stop=(h == 1))
                    mm.then_inc(w1_done, 1)

            def transition(s):
                pe.wait_ge(local_out, s + 1)
                for k in range(KH):
                    pe.wait_ge(h_ready, KH * s + (KH + k + 1))
                    for m in range(2):
                        mm = nc.tensor.matmul(PS[0:HA, 2 + m, 0:PT], W2[:, k, HA * m:HA * m + HA], H1[:, k, :],
                                              start=(k == 0), stop=(k == KH - 1))
                mm.then_inc(w2_done, 1)

            def stats(s, with_a):
                for n in range(2):
                    pe.wait_ge(sq_summed, 2 * s + (n + 2))
                    if n and with_a:
                        pe.wait_ge(topk_step, 5 * s + 10)
                    mm = nc.tensor.matmul(PS[0:HA, 6 + n, 0:PT], ONES[:, 0:HA], SQS[:, n, :], start=True, stop=True)
                mm.then_inc(stats_done, 1)

            def up(k):
                pe.wait_ge(scattered, k + 2)
                for m in range(KC):
                    pe.wait_ge(resid, KC * k + (m + 1))
                    for h in range(2):
                        mm = nc.tensor.matmul(PS[:, 4 + m % 2, 0:PT], UP[:, h, 128 * m:128 * m + 128],
                                              FU[:, k & 1, h, :], start=(h == 0), stop=(h == 1))
                    mm.then_inc(up_done, 1)

            def chain(c):
                pe.wait_ge(resid, KC * PAIRS * c + 2)
                pe.wait_ge(chain_dve, after("dve", c, "tok"))
                for part in range(2):
                    for hd in range(HEADS):
                        col = part * A + hd * DH
                        for h in range(2):
                            mm = nc.tensor.matmul(PS[0:DH, 4 + part, hd * NANC:(hd + 1) * NANC],
                                                  AIN[:, h, col:col + DH], TOK[:, h, :], start=(h == 0), stop=(h == 1))
                mm.then_inc(chain_pe, 1)
                pe.wait_ge(chain_dve, after("dve", c, "q"))
                for h in range(2):
                    mm = nc.tensor.matmul(PS[:, 4, 0:A], TOK[:, h, :], AIN[:, h, 2 * A:3 * A], start=(h == 0), stop=(h == 1))
                mm.then_inc(chain_pe, 1)
                pe.wait_ge(chain_dve, after("dve", c, "k"))
                for hd in range(HEADS):
                    mm = nc.tensor.matmul(PS[:, 5, hd * NANC:(hd + 1) * NANC], QH[:, hd, :], KHD[:, hd, :], start=True, stop=True)
                mm.then_inc(chain_pe, 1)
                pe.wait_ge(chain_act, after("act", c, "v"))
                pe.wait_ge(chain_dve, after("dve", c, "prob"))
                for hd in range(HEADS):
                    mm = nc.tensor.transpose(PS[:, 4, hd * NANC:(hd + 1) * NANC], S[:, hd, :], IDENT)
                mm.then_inc(chain_pe, 1)
                pe.wait_ge(chain_dve, after("dve", c, "turned"))
                for hd in range(HEADS):
                    mm = nc.tensor.matmul(PS[0:DH, 5, hd * NANC:(hd + 1) * NANC], VV[:, hd * DH:(hd + 1) * DH], ST[:, hd, :],
                                          start=True, stop=True)
                mm.then_inc(chain_pe, 1)
                pe.wait_ge(chain_dve, after("dve", c, "mixed"))
                for m in range(2):
                    for hd in range(HEADS):
                        mm = nc.tensor.matmul(PS[0:HA, 4, m * NANC:(m + 1) * NANC], AOUT[:, hd, HA * m:HA * m + HA],
                                              OH[:, hd, :], start=(hd == 0), stop=(hd == HEADS - 1))
                mm.then_inc(chain_pe, 1)
                pe.wait_ge(chain_dve, after("dve", c, "out"))
                for m in range(2):
                    for h in range(2):
                        mm = nc.tensor.matmul(PS[0:HA, 5, m * NANC:(m + 1) * NANC], APR[:, h, HA * m:HA * m + HA],
                                              A1[:, h, :], start=(h == 0), stop=(h == 1))
                mm.then_inc(chain_pe, 1)
                pe.wait_ge(chain_dve, after("dve", c, "ap_scaled"))
                for h in range(2):
                    nc.tensor.matmul(PS[0:HA, 4, 0:NANC], ONES[:, 0:HA], A2[:, h, :], start=(h == 0), stop=(h == 1))
                for m in range(2):
                    for q in range(4):
                        mm = nc.tensor.matmul(PS[0:HA, 4, 256 + m:257 + m], GW1[:, q, HA * m:HA * m + HA],
                                              GIN[:, q:q + 1], start=(q == 0), stop=(q == 3))
                mm.then_inc(chain_pe, 1)
                pe.wait_ge(chain_act, after("act", c, "square"))
                for h in range(2):
                    mm = nc.tensor.matmul(PS[0:HA, 5, 0:NANC], ONES[:, 0:HA], ASQ[:, h, :], start=(h == 0), stop=(h == 1))
                mm.then_inc(chain_pe, 1)
                pe.wait_ge(chain_act, after("act", c, "gelu"))
                for q in range(6):
                    for h in range(2):
                        mm = nc.tensor.matmul(PS[0:HA, 4, 300 + q:301 + q], GW2[:, h, HA * q:HA * q + HA], GH[:, h:h + 1],
                                              start=(h == 0), stop=(h == 1))
                mm.then_inc(chain_pe, 1)

            def back(s, with_a):
                hidden(s, with_a)
                transition(s)
                stats(s, with_a)

            down(0)
            salience(0)
            with pe.Fori(1, PAIRS) as j:
                down(j)
                local(j - 1)
                salience(j)
                back(j - 1, True)
            with pe.Fori(1, B) as b:
                s = b * PAIRS
                down(s)
                local(s - 1)
                salience(s)
                back(s - 1, True)
                chain(b - 1)
                with pe.Fori(1, PAIRS) as j:
                    s = b * PAIRS + j
                    down(s)
                    local(s - 1)
                    up(s - (PAIRS + 1))
                    salience(s)
                    back(s - 1, True)
                up(b * PAIRS - 1)
            s = NPAIR - 1
            local(s)
            back(s, False)
            chain(B - 1)
            with pe.Fori(NPAIR - PAIRS, NPAIR) as k:
                up(k)
            pe.wait_ge(cls_loaded, 32)
            pe.wait_ge(cls_mean, 1)
            WC = XC[0:HA].rearrange("p k n -> p (k n)")[:, 0:2 * C].rearrange("p (h n) -> p h n", h=2)
            for m in range(KC):
                pe.wait_ge(resid, KC * NPAIR + 2)
                if m >= 2:
                    pe.wait_ge(cls_out, m - 1)
                for h in range(2):
                    mm = nc.tensor.matmul(PS[:, 4 + m % 2, 0:B * T], WC[:, h, 128 * m:128 * m + 128], FS[:, h, :],
                                          start=(h == 0), stop=(h == 1))
                mm.then_inc(cls_mm, 1)

        @block.scalar
        def _(act):
            act.sem_inc(h_ready, KH)
            act.sem_inc(trans_out, 1)
            act.wait_ge(setup_pe, 2)
            act.wait_ge(consts_set, 4)
            nc.scalar.activation(W1P[:], PS[0:HA, 0:2, 0:HID], ACT.Identity).then_inc(setup_act, 1)
            act.wait_ge(setup_dve, 7)

            def take_ph(s, j):
                act.wait_ge(xa_used, 2 * s + 4)
                act.wait_ge(gathered, s)
                hold(act, delta_ready, 2 * s)
                for h in range(2):
                    nc.scalar.activation(window(PH, h, ph_base(j & 1)),
                                         PS[0:HA, h, 0:PT].rearrange("p (f r c) -> p f r c", f=2, c=SIDE),
                                         ACT.Identity, bias=vec("down_b")[:, h:h + 1]).then_inc(ph_ready, 1)

            def take_abs(s, b, j):
                act.wait_ge(delta_ready, 2 * s + 2)
                hold(act, abs_summed, s)
                for h in range(2):
                    nc.scalar.activation(AD[:, h, :], DL[:, h, ds(2 * j + 1, 2), :].rearrange("p f n -> p (f n)"), ACT.Abs,
                                         accum_out=DPS[:, h, b & 1, ds(j, 1)]).then_inc(abs_ready, 1)

            def take_local(s, j):
                act.wait_ge(lpw_done, s + 1)
                hold(act, fused, s + 1)
                nc.scalar.activation(NRM[:, 0:2, j, :], halves(2), ACT.Identity).then_inc(local_out, 1)
                act.wait_ge(local_out, s + 1)
                hold(act, sq_summed, 2 * s + 1)
                nc.scalar.activation(SQ[:], NRM[:, 0:2, j, :], ACT.Square).then_inc(sq_ready, 1)

            def gelus(s):
                act.wait_ge(tconv_taps, 6 * s + 6)
                nc.scalar.activation(TV[:], TV[:], ACT.Gelu).then_inc(tconv_gelu, 1)
                act.wait_ge(w2_done, s + 1)
                for m in range(KH):
                    act.wait_ge(w1_done, KH * s + (m + 2))
                    nc.scalar.activation(H1[:, m, :], PS[:, (0, 1, 6)[m], 0:PT], ACT.Gelu,
                                         bias=VP[:, m:m + 1]).then_inc(h_ready, 1)

            def take_transition(s, j):
                hold(act, w2_done, s + 2)
                for h in range(2):
                    nc.scalar.activation(NRM[:, 2 + h, j, :], PS[0:HA, 2 + h, 0:PT], ACT.Identity,
                                         bias=vec("mlp_b2")[:, h:h + 1]).then_inc(trans_out, 1)
                act.wait_ge(trans_out, 2 * s + 3)
                hold(act, sq_summed, 2 * s + 2)
                nc.scalar.activation(SQ[:], NRM[:, 2:4, j, :], ACT.Square).then_inc(sq_ready, 1)

            def conv_gelus(s):
                act.wait_ge(conv_taps, 18 * s + 18)
                act.wait_ge(lpw_done, s)
                for h in range(2):
                    nc.scalar.activation(GL[:, h, :].rearrange("p (f r c) -> p f r c", f=2, c=SIDE),
                                         window(CV, h, 0), ACT.Gelu).then_inc(conv_gelu, 1)

            def rsqrts(s):
                act.wait_ge(stats_done, s + 2)
                act.wait_ge(normed, s + 1)
                nc.scalar.activation(RY[:], halves(6), ACT.Abs_reciprocal_sqrt, bias=EPSC[:]).then_inc(rs_first, 1)
                act.wait_ge(rs_first, s + 1)
                nc.scalar.activation(RT[:], RY[:], ACT.Square).then_inc(rs_square, 1)

            def chain(c):
                act.wait_ge(chain_pe, after("pe", c, "v"))
                nc.scalar.activation(VV[:], PS[:, 4, 0:A], ACT.Identity).then_inc(chain_act, 1)
                act.wait_ge(chain_dve, after("dve", c, "shifted"))
                nc.scalar.activation(S[:], S[:], ACT.Exp).then_inc(chain_act, 1)
                act.wait_ge(chain_dve, after("dve", c, "centred"))
                nc.scalar.activation(ASQ[:], XCN[:], ACT.Square).then_inc(chain_act, 1)
                act.wait_ge(chain_dve, after("dve", c, "gate1"))
                nc.scalar.activation(GH[:], GH[:], ACT.Gelu).then_inc(chain_act, 1)
                act.wait_ge(chain_dve, after("dve", c, "gshift"))
                nc.scalar.activation(GT[:], GT[:], ACT.Exp).then_inc(chain_act, 1)
                act.wait_ge(chain_pe, after("pe", c, "var"))
                nc.scalar.activation(AY[:], PS[0:HA, 5, 0:NANC], ACT.Abs_reciprocal_sqrt, bias=EPSC[:]).then_inc(chain_act, 1)
                act.wait_ge(chain_act, after("act", c, "rsqrt"))
                nc.scalar.activation(AT[:], AY[:], ACT.Square).then_inc(chain_act, 1)

            def back(s, j):
                take_local(s, j)
                gelus(s)
                take_transition(s, j)

            take_ph(0, 0)
            take_abs(0, 0, 0)
            conv_gelus(0)
            with act.Fori(1, PAIRS) as j:
                take_ph(j, j)
                take_abs(j, 0, j)
                back(j - 1, j - 1)
                conv_gelus(j)
                rsqrts(j - 1)
            with act.Fori(1, B) as b:
                s = b * PAIRS
                take_ph(s, 0)
                take_abs(s, b, 0)
                back(s - 1, PAIRS - 1)
                conv_gelus(s)
                chain(b - 1)
                rsqrts(s - 1)
                with act.Fori(1, PAIRS) as j:
                    s = b * PAIRS + j
                    take_ph(s, j)
                    take_abs(s, b, j)
                    back(s - 1, j - 1)
                    conv_gelus(s)
                    rsqrts(s - 1)
            back(NPAIR - 1, PAIRS - 1)
            chain(B - 1)
            rsqrts(NPAIR - 1)

        @block.gpsimd
        def _(pool):
            pool.memset(PH[:], 0.0).then_inc(consts_set, 1)
            pool.memset(DL[:, :, 0, :], 0.0).then_inc(consts_set, 1)
            pool.memset(DL[:, :, T + 1, :], 0.0).then_inc(consts_set, 1)
            for done in (gathered, sq_summed, scattered):
                pool.sem_inc(done, 1)
            pool.wait_ge(consts_set, 4)

            def sum_abs(s):
                pool.wait_ge(abs_ready, 2 * s + 2)
                pool.wait_ge(sal_ready, s)
                nc.gpsimd.tensor_tensor(ADS[:], AD[:, 0, :], AD[:, 1, :], ALU.add).then_inc(abs_summed, 1)

            def sum_squares(s, n):
                pool.wait_ge(sq_ready, 2 * s + (n + 1))
                pool.wait_ge(stats_done, s + 1)
                nc.gpsimd.tensor_tensor(SQS[:, n, :], SQ[:, 0, :], SQ[:, 1, :], ALU.add).then_inc(sq_summed, 1)

            def gather(s, b, j):
                pool.wait_ge(topk_step, 5 * s + 5)
                for f in range(2):
                    for r in range(TOPK):
                        token = pool.value_load(IDX[0:1, s & (2 * PAIRS - 1), f * TOPK + r:f * TOPK + r + 1],
                                                min_val=0, max_val=HW - 1)
                        row = (token * 4682) >> 16
                        col = (2 * j + f) * TOPK + r
                        nc.gpsimd.tensor_copy(G[:, b & 1, 0:2, ds(col, 1)],
                                              PH[:, :, ds(token + row + ((j & 1) * (2 * FP) + (GUARD + f * FP)), 1)])
                        last = nc.gpsimd.tensor_copy(G[:, b & 1, 2:4, ds(col, 1)],
                                                     DL[:].rearrange("p h f n -> p h (f n)")[:, :, ds(token + (2 * j + (f + 1)) * HW, 1)])
                last.then_inc(gathered, 1)

            def scatter(k, j):
                pool.wait_ge(fused, k + (PAIRS + 1))
                for f in range(2):
                    for r in range(TOPK):
                        token = pool.value_load(IDX[0:1, k & (2 * PAIRS - 1), f * TOPK + r:f * TOPK + r + 1],
                                                min_val=0, max_val=HW - 1)
                        at = FU[:, k & 1, :, ds(token + f * HW, 1)]
                        last = nc.gpsimd.tensor_tensor(at, at, Z[:, :, ds((2 * j + f) * TOPK + r, 1)], ALU.add)
                last.then_inc(scattered, 1)

            sum_abs(0)
            gather(0, 0, 0)
            with pool.Fori(1, PAIRS) as j:
                sum_abs(j)
                sum_squares(j - 1, 0)
                gather(j, 0, j)
                sum_squares(j - 1, 1)
            with pool.Fori(1, B) as b:
                s = b * PAIRS
                sum_abs(s)
                sum_squares(s - 1, 0)
                gather(s, b, 0)
                sum_squares(s - 1, 1)
                scatter(s - PAIRS, 0)
                with pool.Fori(1, PAIRS) as j:
                    s = b * PAIRS + j
                    sum_abs(s)
                    sum_squares(s - 1, 0)
                    gather(s, b, j)
                    sum_squares(s - 1, 1)
                    scatter(s - PAIRS, j)
            sum_squares(NPAIR - 1, 0)
            sum_squares(NPAIR - 1, 1)
            with pool.Fori(0, PAIRS) as j:
                scatter(NPAIR - PAIRS + j, j)

        @block.vector
        def _(dve):
            v = nc.vector
            dve.sem_inc(newton_a, 1)
            dve.sem_inc(normed, 1)
            dve.sem_inc(fused, PAIRS)
            dve.sem_inc(resid, 2)
            dve.sem_inc(up_done, 2 * KC)
            v.memset(EPSC[:], EPS)
            v.memset(ONES[:], 1.0 / A).then_inc(consts_set, 1)
            dve.wait_ge(consts_set, 4)
            dve.wait_ge(wts_loaded, 16 * (WEIGHT_LOADS - 1))
            v.tensor_reduce(WM[0:HA, 0:2], LPW, AX.X, ALU.add)
            v.tensor_reduce(WM[:, 2:2 + KH], W2[:], AX.X, ALU.add).then_inc(setup_dve, 1)
            dve.wait_ge(setup_dve, 1)
            v.tensor_scalar(WM[:, 2:2 + KH], WM[:, 2:2 + KH], 1.0 / A, None, ALU.mult).then_inc(setup_dve, 1)
            v.tensor_scalar(WM[0:HA, 0:2], WM[0:HA, 0:2], 1.0 / A, None, ALU.mult).then_inc(setup_dve, 1)
            dve.wait_ge(setup_dve, 3)
            for h in range(2):
                v.tensor_scalar(LPW[:, h, :], LPW[:, h, :], WM[0:HA, h:h + 1], None, ALU.subtract)
            for k in range(KH):
                v.tensor_scalar(W2[:, k, :], W2[:, k, :], WM[:, 2 + k:3 + k], None, ALU.subtract).then_inc(setup_dve, 1)
            dve.wait_ge(setup_pe, 3)
            v.tensor_tensor(vec("mlp_b2"), vec("mlp_b2"), PS[0:HA, 2, 0:1].to_broadcast([HA, 2]), ALU.subtract).then_inc(setup_dve, 1)

            def delta(s, b, j):
                dve.wait_ge(ph_ready, 2 * s + 2)
                here = ph_base(j & 1)
                before = here if isinstance(j, int) and j == 0 else ph_base(1 - (j & 1)) + FP
                for f, prev in ((0, before), (1, here)):
                    v.tensor_tensor(DL[:, :, ds(2 * j + 1 + f, 1), :].rearrange("p h f (r c) -> p h (f r) c", c=SIDE),
                                    frame2(PH, here + f * FP), frame2(PH, prev), ALU.subtract).then_inc(delta_ready, 1)

            def tconv(s, j, with_a=True):
                dve.wait_ge(w1_done, KH * s + 1)
                dve.wait_ge(delta_ready, 2 * s + (4 if with_a else 2))
                for k in range(3):
                    for h in range(2):
                        src = DL[:, h, ds(2 * j + k, 2), :].rearrange("p f n -> p (f n)")
                        if k == 0:
                            tap = v.tensor_scalar(TV[:, h, :], src, TDW[:, h, 0:1], None, ALU.mult)
                        else:
                            dve.wait_ge(tconv_taps, 6 * s + (2 * k + h - 1))
                            tap = v.scalar_tensor_tensor(out=TV[:, h, :], in0=src, scalar=TDW[:, h, k:k + 1],
                                                         in1=TV[:, h, :], op0=ALU.mult, op1=ALU.add)
                        tap.then_inc(tconv_taps, 1)

            def conv_tap(s, j, k):
                off = (k // 3 - 1) * PITCH + (k % 3 - 1)
                for h in range(2):
                    src, dst = rows(PH, h, ph_base(j & 1) + off), rows(CV, h, 0)
                    if k == 0:
                        if h == 0:
                            dve.wait_ge(conv_gelu, 2 * s)
                        tap = v.tensor_scalar(dst, src, LDW[:, h, 0:1], None, ALU.mult)
                    else:
                        dve.wait_ge(conv_taps, 18 * s + (2 * k + h - 1))
                        tap = v.scalar_tensor_tensor(out=dst, in0=src, scalar=LDW[:, h, k:k + 1], in1=dst,
                                                     op0=ALU.mult, op1=ALU.add)
                    tap.then_inc(conv_taps, 1)

            def frame_sums(k):
                dve.wait_ge(scattered, k + 2)
                v.tensor_reduce(FS[:, :, ds(2 * k, 2)], FU[:, k & 1, :, :].rearrange("p h (f n) -> p h f n", f=2), AX.X, ALU.add)

            def residual(k, m):
                dve.wait_ge(up_done, KC * k + (m + 1 + 2 * KC))
                if m % HK == 0:
                    dve.wait_ge(xc_loaded[m // HK], 16 * k + 16)
                v.scalar_tensor_tensor(out=XC[:, m, :], in0=PS[:, 4 + m % 2, 0:PT], scalar=VP[:, KH + m:KH + m + 1],
                                       in1=XC[:, m, :], op0=ALU.add, op1=ALU.add).then_inc(resid, 1)

            def topk(s):
                hold(dve, sal_ready, s + 1)
                for f in range(2):
                    sal = PS[0:1, 7, f * HW:(f + 1) * HW]
                    v.max(MX[:, f, :], sal).then_inc(topk_step, 1)
                for f in range(2):
                    sal = PS[0:1, 7, f * HW:(f + 1) * HW]
                    hold(dve, topk_step, 5 * s + 2)
                    v.max_index(IDN[:, f * TOPK:(f + 1) * TOPK], MX[:, f, :], sal).then_inc(topk_step, 1)
                dve.wait_ge(topk_step, 5 * s + 4)
                v.tensor_copy(IDX[0:1, s & (2 * PAIRS - 1), :], IDN[:]).then_inc(topk_step, 1)

            def fuse(k, j):
                dve.wait_ge(up_done, KC * k + KC)
                for h in range(2):
                    v.tensor_scalar(FT[:, h, :], NRM[:, 2 + h, j, :], GG[:, 2 + h:3 + h], GC[:, h:h + 1],
                                    ALU.mult, ALU.add).then_inc(weighted, 1)
                for h in range(2):
                    dve.wait_ge(weighted, 2 * k + (h + 1))
                    last = v.scalar_tensor_tensor(out=FU[:, k & 1, h, :], in0=NRM[:, h, j, :], scalar=GG[:, h:h + 1],
                                                  in1=FT[:, h, :], op0=ALU.mult, op1=ALU.add)
                last.then_inc(fused, 1)

            def finalize(s, j):
                dve.wait_ge(rs_square, s + 1)
                v.scalar_tensor_tensor(out=RT[:], in0=halves(6), scalar=EPSC[:], in1=RT[:],
                                       op0=ALU.add, op1=ALU.mult).then_inc(newton_a, 1)
                dve.wait_ge(newton_a, s + 2)
                v.tensor_scalar(RT[:], RT[:], -0.5, 1.5, ALU.mult, ALU.add).then_inc(newton_b, 1)
                dve.wait_ge(newton_b, s + 1)
                v.tensor_tensor(RY[:], RY[:], RT[:], ALU.mult).then_inc(newton_c, 1)
                dve.wait_ge(newton_c, s + 1)
                for n in range(2):
                    last = v.tensor_tensor(NRM[:, 2 * n:2 * n + 2, j, :], NRM[:, 2 * n:2 * n + 2, j, :],
                                           RY[:, n:n + 1, :].to_broadcast([HA, 2, PT]), ALU.mult)
                last.then_inc(normed, 1)

            def chain(c):
                def done(instruction, step):
                    instruction.then_inc(chain_dve, 1)
                    dve.wait_ge(chain_dve, after("dve", c, step))

                done(v.tensor_reduce(GIN[:, 0:2], DPS[:, :, c & 1, :], AX.X, ALU.add), "dp")
                done(v.tensor_scalar(GIN[:, 0:2], GIN[:, 0:2], 1.0 / (T * HW), None, ALU.mult), "dp_scaled")
                dve.wait_ge(gathered, PAIRS * c + (PAIRS + 1))
                done(v.tensor_tensor(TOK[:], G[:, c & 1, 0:2, :], G[:, c & 1, 2:4, :], ALU.add), "tok")
                dve.wait_ge(chain_pe, after("pe", c, "qk"))
                for part, dst, step in ((0, QH, "q"), (1, KHD, "k")):
                    done(v.tensor_tensor(dst[:], PS[0:DH, 4 + part, 0:HEADS * NANC].rearrange("p (h n) -> p h n", h=HEADS),
                                         VH[:, part, :].unsqueeze(2).to_broadcast([DH, HEADS, NANC]), ALU.add), step)
                dve.wait_ge(chain_pe, after("pe", c, "scores"))
                done(v.scalar_tensor_tensor(out=S[:], in0=PS[:, 5, 0:HEADS * NANC].rearrange("p (h n) -> p h n", h=HEADS),
                                            scalar=float(DH) ** -0.5,
                                            in1=MASK.unsqueeze(1).to_broadcast([NANC, HEADS, NANC]),
                                            op0=ALU.mult, op1=ALU.add), "masked")
                done(v.tensor_reduce(SM[:, 0, :], S[:], AX.X, ALU.max), "max")
                done(v.tensor_tensor(S[:], S[:], SM[:, 0, :].unsqueeze(2).to_broadcast([NANC, HEADS, NANC]),
                                     ALU.subtract), "shifted")
                dve.wait_ge(chain_act, after("act", c, "exp"))
                done(v.tensor_reduce(SM[:, 1, :], S[:], AX.X, ALU.add), "sum")
                done(v.reciprocal(SM[:, 2, :], SM[:, 1, :]), "recip")
                done(v.tensor_tensor(S[:], S[:], SM[:, 2, :].unsqueeze(2).to_broadcast([NANC, HEADS, NANC]),
                                     ALU.mult), "prob")
                dve.wait_ge(chain_pe, after("pe", c, "turned"))
                done(v.tensor_copy(ST[:], PS[:, 4, 0:HEADS * NANC].rearrange("p (h n) -> p h n", h=HEADS)), "turned")
                dve.wait_ge(chain_pe, after("pe", c, "mixed"))
                done(v.tensor_tensor(OH[:], PS[0:DH, 5, 0:HEADS * NANC].rearrange("p (h n) -> p h n", h=HEADS),
                                     VH[:, 2, :].unsqueeze(2).to_broadcast([DH, HEADS, NANC]), ALU.add), "mixed")
                for bank, dst, bias, step in ((4, A1, "out_b", "out"), (5, A2, "proj_b", "anchor")):
                    dve.wait_ge(chain_pe, after("pe", c, step))
                    done(v.tensor_tensor(dst[:], PS[0:HA, bank, 0:2 * NANC].rearrange("p (h n) -> p h n", h=2),
                                         vec(bias).unsqueeze(2).to_broadcast([HA, 2, NANC]), ALU.add), step)
                done(v.tensor_reduce(GIN[:, 2:4], A2[:], AX.X, ALU.add), "ap")
                done(v.tensor_scalar(GIN[:, 2:4], GIN[:, 2:4], 1.0 / NANC, None, ALU.mult), "ap_scaled")
                dve.wait_ge(chain_pe, after("pe", c, "mean_gate1"))
                done(v.tensor_tensor(XCN[:], A2[:], PS[0:HA, 4, 0:NANC].unsqueeze(1).to_broadcast([HA, 2, NANC]),
                                     ALU.subtract), "centred")
                done(v.tensor_tensor(GH[:], vec("gate_b1"), PS[0:HA, 4, 256:258], ALU.add), "gate1")
                dve.wait_ge(chain_pe, after("pe", c, "gate2"))
                done(v.tensor_tensor(GT[:], vec("gate_b2"), PS[0:HA, 4, 300:306], ALU.add), "gate2")
                done(v.tensor_tensor(GM[:], GT[:, 0:2], GT[:, 2:4], ALU.max), "gmax1")
                done(v.tensor_tensor(GM[:], GM[:], GT[:, 4:6], ALU.max), "gmax2")
                three = [HA, 3, 2]
                g3 = GT[:].rearrange("p (g h) -> p g h", h=2)
                done(v.tensor_tensor(g3, g3, GM[:].unsqueeze(1).to_broadcast(three), ALU.subtract), "gshift")
                dve.wait_ge(chain_act, after("act", c, "gate_exp"))
                done(v.tensor_tensor(GM[:], GT[:, 0:2], GT[:, 2:4], ALU.add), "gsum1")
                done(v.tensor_tensor(GM[:], GM[:], GT[:, 4:6], ALU.add), "gsum2")
                done(v.reciprocal(GM[:], GM[:]), "grecip")
                done(v.tensor_tensor(g3, g3, GM[:].unsqueeze(1).to_broadcast(three), ALU.mult), "gates")
                done(v.tensor_tensor(GG[:], GT[:], vec("gain"), ALU.mult), "gains")
                done(v.tensor_tensor(GB[:], GT[:], vec("beta"), ALU.mult), "betas")
                done(v.tensor_tensor(GC[:], GB[:, 0:2], GB[:, 2:4], ALU.add), "const1")
                done(v.tensor_tensor(GC[:], GC[:], GB[:, 4:6], ALU.add), "const2")
                dve.wait_ge(chain_act, after("act", c, "rsqrt_sq"))
                done(v.scalar_tensor_tensor(out=AT[:], in0=PS[0:HA, 5, 0:NANC], scalar=EPSC[:], in1=AT[:],
                                            op0=ALU.add, op1=ALU.mult), "newton1")
                done(v.tensor_scalar(AT[:], AT[:], -0.5, 1.5, ALU.mult, ALU.add), "newton2")
                done(v.tensor_tensor(AY[:], AY[:], AT[:], ALU.mult), "newton3")
                dve.wait_ge(scattered, PAIRS * c + 1)
                done(v.tensor_tensor(Z[:], XCN[:], AY[:].unsqueeze(1).to_broadcast([HA, 2, NANC]), ALU.mult), "znorm")
                done(v.tensor_tensor(Z[:], Z[:], GG[:, 4:6].unsqueeze(2).to_broadcast([HA, 2, NANC]), ALU.mult), "z")

            def finish_and_conv(k, s, j):
                frame_sums(k)
                for m in range(KC):
                    residual(k, m)
                    if s is not None:
                        conv_tap(s, j, m)
                if s is not None:
                    for m in range(KC, 9):
                        conv_tap(s, j, m)

            delta(0, 0, 0)
            topk(0)
            for m in range(9):
                conv_tap(0, 0, m)
            with dve.Fori(1, PAIRS) as j:
                delta(j, 0, j)
                tconv(j - 1, j - 1)
                topk(j)
                for m in range(9):
                    conv_tap(j, j, m)
                finalize(j - 1, j - 1)
            with dve.Fori(1, B) as b:
                s = b * PAIRS
                delta(s, b, 0)
                tconv(s - 1, PAIRS - 1)
                topk(s)
                for m in range(9):
                    conv_tap(s, 0, m)
                chain(b - 1)
                fuse(s - PAIRS, 0)
                finalize(s - 1, PAIRS - 1)
                with dve.Fori(1, PAIRS) as j:
                    s = b * PAIRS + j
                    delta(s, b, j)
                    tconv(s - 1, j - 1)
                    finish_and_conv(s - (PAIRS + 1), s, j)
                    topk(s)
                    fuse(s - PAIRS, j)
                    finalize(s - 1, j - 1)
                finish_and_conv(b * PAIRS - 1, None, None)
            tconv(NPAIR - 1, PAIRS - 1, False)
            chain(B - 1)
            fuse(NPAIR - PAIRS, 0)
            finalize(NPAIR - 1, PAIRS - 1)
            with dve.Fori(1, PAIRS) as j:
                fuse(NPAIR - PAIRS + j, j)
                finish_and_conv(NPAIR - PAIRS - 1 + j, None, None)
            finish_and_conv(NPAIR - 1, None, None)
            v.tensor_scalar(FS[:], FS[:], 1.0 / HW, None, ALU.mult).then_inc(cls_mean, 1)
            XK = XA[:].rearrange("p k n -> p (k n)")[:, 0:KC * B * T].rearrange("p (k n) -> p k n", k=KC)
            dve.wait_ge(cls_loaded, 32)
            for m in range(KC):
                dve.wait_ge(cls_mm, m + 1)
                v.scalar_tensor_tensor(out=XK[:, m, :], in0=PS[:, 4 + m % 2, 0:B * T],
                                       scalar=VP[:, KH + KC + m:KH + KC + m + 1], in1=XK[:, m, :],
                                       op0=ALU.add, op1=ALU.add).then_inc(cls_out, 1)


def kernel(**inputs):
    import numpy as np
    import concourse.bacc as bacc
    from concourse.bass_utils import run_bass_kernel_spmd

    a = {k.replace("L0_conv_", ""): np.asarray(v) for k, v in inputs.items()}
    x = a["x"]

    def by(n, w):
        k = w.shape[0] // n
        return w.reshape(k, n, *w.shape[1:]).swapaxes(0, 1)

    def flat(w):
        return w.reshape(w.shape[0], -1)

    vectors = {"down_b": by(HA, a["down_b"]), "mlp_b2": by(HA, a["tmlp_b2"]), "out_b": by(HA, a["attn_out_b"]),
               "gain": np.concatenate([by(HA, a[n]) for n in ("lnorm_g", "tnorm_g", "anorm_g")], 1),
               "beta": np.concatenate([by(HA, a[n]) for n in ("lnorm_b", "tnorm_b", "anorm_b")], 1),
               "proj_b": by(HA, a["aproj_b"]), "gate_b1": by(HA, a["gate_b1"]), "gate_b2": by(HA, a["gate_b2"]),
               "ldw": flat(by(HA, a["ldw_w"].reshape(A, 9))), "tdw": flat(by(HA, a["tdw_w"].reshape(A, 3)))}
    weights = {"lpw": a["lpw_w"], "up": a["up_w"], "attn_in": a["attn_in_w"], "aproj": a["aproj_w"],
               "gate1": a["gate_w1"], "gate2": a["gate_w2"]}
    place = np.arange(NANC)
    mask = np.where((place[:, None] - place[None, :]) % TOPK == 0, 0.0, -1e30)
    arrays = {
        "xp": x[:, :, 1:, :].reshape(B, PAIRS, 2, HW, KC, 128).transpose(0, 1, 5, 4, 2, 3).reshape(NPAIR, 128, KC, PT),
        "xcls": x[:, :, 0, :].reshape(B * T, KC, 128).transpose(2, 1, 0).reshape(128, KC * B * T),
        "wdown": by(128, a["down_w"].T),
        "w96": np.concatenate([flat(by(HA, weights[n].T)) for n in W96], 1),
        "wsetup": np.concatenate([flat(by(HA, a["tpw_w"])), flat(by(HA, a["tmlp_w1"].T))], 1),
        "wcls": flat(by(HA, a["cls_w"].T)),
        "w2": by(128, a["tmlp_w2"].T),
        "aout": by(DH, a["attn_out_w"].T),
        "v96": np.concatenate([vectors[n] for n in V96], 1),
        "v48": a["attn_in_b"].reshape(3, HEADS, DH).transpose(2, 0, 1),
        "v128": np.concatenate([by(128, a[n]) for n in ("tmlp_b1", "up_b", "cls_b")], 1),
        "consts": np.stack([np.eye(128), mask], 1).astype(np.float32),
    }
    arrays = {k: np.ascontiguousarray(v, dtype=np.float32) for k, v in arrays.items()}
    nc = bacc.Bacc("TRN2", target_bir_lowering=False, num_devices=1)
    args = [nc.dram_tensor(k, v.shape, F32, kind="ExternalInput").ap() for k, v in arrays.items()]
    args.append(nc.dram_tensor("out", (NPAIR, 128, KC, PT), F32, kind="ExternalOutput").ap())
    args.append(nc.dram_tensor("outcls", (128, KC * B * T), F32, kind="ExternalOutput").ap())
    build(nc, *args)
    r = run_bass_kernel_spmd(nc, [arrays], core_ids=[0]).results[0]
    patch = r["out"].reshape(B, PAIRS, 128, KC, 2, HW).transpose(0, 1, 4, 5, 3, 2).reshape(B, T, HW, C)
    cls = r["outcls"].reshape(128, KC, B * T).transpose(2, 1, 0).reshape(B, T, 1, C)
    return np.concatenate([cls, patch], 2)
```

```python
from contextlib import ExitStack

import concourse.bass as bass
from concourse import mybir

F32 = mybir.dt.float32
U32 = mybir.dt.uint32
ACT = mybir.ActivationFunctionType
ALU = mybir.AluOpType
AX = mybir.AxisListType

B, T, SIDE, C, A = 16, 16, 14, 768, 192
HW = SIDE * SIDE
PT = 2 * HW
HA = A // 2
KC = C // 128
PAIRS = T // 2
NPAIR = B * PAIRS
HID = 2 * A
KH = HID // 128
TOPK, HEADS = 8, 4
DH = A // HEADS
NANC = T * TOPK
EPS = 1e-5
PITCH = SIDE + 1
FP = PITCH * PITCH
GUARD = PITCH + 1
ROWS = 2 * SIDE + 1
SPAN = ROWS * PITCH

V96 = {}
_at = 0
for _name, _n in (("down_b", 2), ("gain", 6), ("beta", 6), ("mlp_b2", 2), ("out_b", 2), ("proj_b", 2),
                  ("gate_b1", 2), ("gate_b2", 6), ("ldw", 18), ("tdw", 6)):
    V96[_name] = (_at, _n)
    _at += _n
NV96 = _at
W96 = {}
_at = 0
for _name, _n in (("lpw", 2 * A), ("up", 2 * C), ("attn_in", 2 * 3 * A), ("aproj", 2 * A),
                  ("gate1", 4 * A), ("gate2", 2 * 3 * A)):
    W96[_name] = (_at, _n)
    _at += _n
NW96 = _at
NSETUP = 2 * A + 2 * HID

CHAIN = {
    "pe": ["qk", "v", "scores", "turned", "mixed", "out", "anchor", "mean_gate1", "var", "gate2"],
    "act": ["v", "exp", "square", "gelu", "gate_exp", "rsqrt", "rsqrt_sq"],
    "dve": ["dp", "dp_scaled", "tok", "q", "k", "masked", "max", "shifted", "sum", "recip", "prob",
            "turned", "mixed", "out", "anchor", "ap", "ap_scaled", "centred", "gate1", "gate2",
            "gmax1", "gmax2", "gshift", "gsum1", "gsum2", "grecip", "gates", "gains", "betas",
            "const1", "const2", "newton1", "newton2", "newton3", "znorm", "z"],
}


def after(engine, clip, step):
    steps = CHAIN[engine]
    return clip * len(steps) + (steps.index(step) + 1)


def build(nc, xp, xcls, wdown, w96, wsetup, wcls, w2, aout, v96, v48, v128, consts, out, outcls):
    ds = bass.ds
    with ExitStack() as ctx:
        def sb(name, shape, dt=F32):
            return ctx.enter_context(nc.sbuf_tensor(name, shape, dt))

        def sem(name):
            return ctx.enter_context(nc.semaphore(name))

        WD = sb("WD", [128, KC, A])
        W = sb("W", [HA, NW96])
        W1P = sb("W1P", [HA, 2, HID])
        W2 = sb("W2", [128, KH, A])
        AOUT = sb("AOUT", [DH, HEADS, A])
        VA = sb("VA", [HA, NV96])
        VH = sb("VH", [DH, 3, HEADS])
        VP = sb("VP", [128, KH + 2 * KC])
        CST = sb("CST", [128, 2, 128])
        ONES = sb("ONES", [HA, 128])
        EPSC = sb("EPSC", [HA, 1])
        WM = sb("WM", [128, 8])

        def wt(name, n):
            a, m = W96[name]
            return W[:, a:a + m].rearrange("p (k n) -> p k n", n=n)

        def vec(name):
            a, m = V96[name]
            return VA[:, a:a + m]

        LPW, UP, AIN = wt("lpw", A), wt("up", C), wt("attn_in", 3 * A)
        APR, GW1, GW2 = wt("aproj", A), wt("gate1", A), wt("gate2", 3 * A)
        LDW = vec("ldw").rearrange("p (h k) -> p h k", k=9)
        TDW = vec("tdw").rearrange("p (h k) -> p h k", k=3)
        IDENT, MASK = CST[:, 0, :], CST[:, 1, :]

        XA = sb("XA", [128, KC, PT])
        XC = sb("XC", [128, KC, PT])
        PH = sb("PH", [HA, 2, GUARD + 4 * FP + 2])
        DL = sb("DL", [HA, 2, T + 2, HW])
        NRM = sb("NRM", [HA, 4, PAIRS, PT])
        CV = sb("CV", [HA, 2, 2 * FP])
        TV = sb("TV", [HA, 2, PT])
        GL = sb("GL", [HA, 2, PT])
        H1 = sb("H1", [128, KH, PT])
        AD = sb("AD", [HA, 2, PT])
        PD = sb("PD", [HA, 2, 2, PT])
        ADS = sb("ADS", [HA, PT])
        SQ = sb("SQ", [HA, 2, PT])
        SQS = sb("SQS", [HA, 2, PT])
        RY = sb("RY", [HA, 2, PT])
        RT = sb("RT", [HA, 2, PT])
        FT = sb("FT", [HA, 2, PT])
        FU = sb("FU", [HA, 2, 2, PT])
        FS = sb("FS", [HA, 2, B * T])
        MX = sb("MX", [1, 2, TOPK])
        IDN = sb("IDN", [1, 2 * TOPK], U32)
        IDX = sb("IDX", [1, 2 * PAIRS, 2 * TOPK], U32)
        DPS = sb("DPS", [HA, 2, 2, PAIRS])
        G = sb("G", [HA, 2, 2, NANC])
        TOK = sb("TOK", [HA, 2, NANC])
        QH = sb("QH", [DH, HEADS, NANC])
        KHD = sb("KHD", [DH, HEADS, NANC])
        VV = sb("VV", [NANC, A])
        S = sb("S", [NANC, HEADS, NANC])
        ST = sb("ST", [NANC, HEADS, NANC])
        SM = sb("SM", [NANC, 3, HEADS])
        OH = sb("OH", [DH, HEADS, NANC])
        A1 = sb("A1", [HA, 2, NANC])
        A2 = sb("A2", [HA, 2, NANC])
        XCN = sb("XCN", [HA, 2, NANC])
        ASQ = sb("ASQ", [HA, 2, NANC])
        AY = sb("AY", [HA, NANC])
        AT = sb("AT", [HA, NANC])
        Z = sb("Z", [HA, 2, NANC])
        GIN = sb("GIN", [HA, 4])
        GH = sb("GH", [HA, 2])
        GT = sb("GT", [HA, 6])
        GM = sb("GM", [HA, 2])
        GG = sb("GG", [HA, 6])
        GB = sb("GB", [HA, 6])
        GC = sb("GC", [HA, 2])

        PS = ctx.enter_context(nc.psum_tensor("PS", [128, 8, 512], F32))

        wts_loaded = sem("wts_loaded")
        consts_set = sem("consts_set")
        holds = sem("holds")
        setup_pe = sem("setup_pe")
        setup_dve = sem("setup_dve")
        setup_act = sem("setup_act")
        xa_loaded = [sem(f"xa_loaded{h}") for h in range(2)]
        xc_loaded = [sem(f"xc_loaded{h}") for h in range(2)]
        stored = [sem(f"stored{h}") for h in range(2)]
        xa_used = sem("xa_used")
        ph_ready = sem("ph_ready")
        delta_ready = sem("delta_ready")
        ph_delta = sem("ph_delta")
        abs_ready = sem("abs_ready")
        abs_summed = sem("abs_summed")
        sal_ready = sem("sal_ready")
        topk_step = sem("topk_step")
        gathered = sem("gathered")
        conv_taps = sem("conv_taps")
        conv_gelu = sem("conv_gelu")
        tconv_taps = sem("tconv_taps")
        tconv_gelu = sem("tconv_gelu")
        lpw_done = sem("lpw_done")
        local_out = sem("local_out")
        sq_ready = sem("sq_ready")
        sq_summed = sem("sq_summed")
        w1_done = sem("w1_done")
        h_ready = sem("h_ready")
        w2_done = sem("w2_done")
        trans_out = sem("trans_out")
        stats_done = sem("stats_done")
        rs_first = sem("rs_first")
        rs_square = sem("rs_square")
        newton_a = sem("newton_a")
        newton_b = sem("newton_b")
        newton_c = sem("newton_c")
        normed = sem("normed")
        weighted = sem("weighted")
        fused = sem("fused")
        scattered = sem("scattered")
        up_done = sem("up_done")
        resid = sem("resid")
        chain_pe = sem("chain_pe")
        chain_act = sem("chain_act")
        chain_dve = sem("chain_dve")
        cls_loaded = sem("cls_loaded")
        cls_mean = sem("cls_mean")
        cls_mm = sem("cls_mm")
        cls_out = sem("cls_out")
        cls_stored = sem("cls_stored")

        block = ctx.enter_context(nc.Block())

        WEIGHT_LOADS = 10

        def hold(eng, semaphore, value):
            eng.wait_ge(semaphore, value)
            eng.sem_inc(holds, 1)

        HK = KC // 2

        def halves(bank, n=PT, p=HA):
            return PS[0:p, bank:bank + 2, 0:n]

        def ph_base(slot):
            return GUARD + slot * (2 * FP)

        def window(tile, half, start, frames=2):
            v = tile[:, half, ds(start, frames * FP)]
            return v.rearrange("p (f r c) -> p f r c", r=PITCH, c=PITCH)[:, :, 0:SIDE, 0:SIDE]

        def frame2(tile, start):
            v = tile[:, :, ds(start, FP)]
            return v.rearrange("p h (r c) -> p h r c", c=PITCH)[:, :, 0:SIDE, 0:SIDE]

        def rows(tile, half, start):
            v = tile[:, half, ds(start, SPAN)]
            return v.rearrange("p (r c) -> p r c", c=PITCH)[:, :, 0:SIDE]

        @block.sync
        def _(sp):
            for h in range(2):
                sp.sem_inc(stored[h], 16)
            for dst, src in ((WD[:], wdown), (W[:], w96), (XC[0:HA].rearrange("p k n -> p (k n)")[:, 0:NSETUP], wsetup),
                             (W2[:], w2), (AOUT[:], aout), (VA[:], v96), (VH[:], v48), (VP[:], v128),
                             (CST[:], consts)):
                sp.dma_start(dst, src).then_inc(wts_loaded, 16)

            def load_xa(s):
                for h in range(2):
                    sp.wait_ge(xa_used, 2 * s + (h + 1))
                    sp.dma_start(XA[:, HK * h:HK * h + HK, :], xp[s, :, HK * h:HK * h + HK, :]).then_inc(xa_loaded[h], 16)

            def load_xc(k):
                for h in range(2):
                    sp.wait_ge(stored[h], 16 * k + 16)
                    sp.dma_start(XC[:, HK * h:HK * h + HK, :], xp[k, :, HK * h:HK * h + HK, :]).then_inc(xc_loaded[h], 16)

            def store(k):
                for h in range(2):
                    sp.wait_ge(resid, KC * k + (HK * (h + 1) + 2))
                    sp.dma_start(out[k, :, HK * h:HK * h + HK, :], XC[:, HK * h:HK * h + HK, :]).then_inc(stored[h], 16)

            AHEAD = PAIRS + 2
            for s in range(AHEAD):
                load_xa(s)
                if s == 1:
                    sp.wait_ge(setup_pe, 2)
            with sp.Fori(0, NPAIR - AHEAD) as k:
                load_xc(k)
                load_xa(k + AHEAD)
                store(k)
            with sp.Fori(NPAIR - AHEAD, NPAIR) as k:
                load_xc(k)
                store(k)
            sp.wait_ge(xa_used, 2 * NPAIR + 2)
            sp.dma_start(XA[:].rearrange("p k n -> p (k n)")[:, 0:KC * B * T], xcls).then_inc(cls_loaded, 16)
            for h in range(2):
                sp.wait_ge(stored[h], 16 * NPAIR + 16)
            sp.dma_start(XC[0:HA].rearrange("p k n -> p (k n)")[:, 0:2 * C], wcls).then_inc(cls_loaded, 16)
            sp.wait_ge(cls_out, KC)
            sp.dma_start(outcls, XA[:].rearrange("p k n -> p (k n)")[:, 0:KC * B * T]).then_inc(cls_stored, 16)
            sp.wait_ge(cls_stored, 16)

        @block.tensor
        def _(pe):
            setup = XC[0:HA].rearrange("p k n -> p (k n)")
            TPW = setup[:, 0:2 * A].rearrange("p (h c) -> p h c", h=2)
            W1T = setup[:, 2 * A:NSETUP].rearrange("p (h n) -> p h n", h=2)
            pe.wait_ge(wts_loaded, 16 * (WEIGHT_LOADS - 1))
            pe.wait_ge(consts_set, 4)
            for m in range(2):
                for h in range(2):
                    mm = nc.tensor.matmul(PS[0:HA, m, 0:HID], TPW[:, h, HA * m:HA * m + HA], W1T[:, h, :],
                                          start=(h == 0), stop=(h == 1))
                mm.then_inc(setup_pe, 1)
            b2 = vec("mlp_b2")
            for h in range(2):
                mm = nc.tensor.matmul(PS[0:HA, 2, 0:1], ONES[:, 0:HA], b2[:, h:h + 1], start=(h == 0), stop=(h == 1))
            mm.then_inc(setup_pe, 1)
            pe.sem_inc(xa_used, 2)
            for done in (w1_done, w2_done, stats_done):
                pe.sem_inc(done, 1)
            pe.wait_ge(setup_act, 1)
            pe.wait_ge(setup_dve, 7)

            def down_start(s):
                pe.wait_ge(h_ready, KH * s)

            def down_blocks(s, blocks):
                for k in blocks:
                    if k % HK == 0:
                        pe.wait_ge(xa_loaded[k // HK], 16 * s + 16)
                    for m in range(2):
                        mm = nc.tensor.matmul(PS[0:HA, m, 0:PT], WD[:, k, HA * m:HA * m + HA], XA[:, k, :],
                                              start=(k == 0), stop=(k == KC - 1))
                    if k % HK == HK - 1:
                        mm.then_inc(xa_used, 1)

            def down(s):
                down_start(s)
                down_blocks(s, range(KC))

            def local(s):
                pe.wait_ge(conv_gelu, 2 * s + 2)
                pe.wait_ge(trans_out, 2 * s + 1)
                for m in range(2):
                    for h in range(2):
                        mm = nc.tensor.matmul(PS[0:HA, 2 + m, 0:PT], LPW[:, h, HA * m:HA * m + HA], GL[:, h, :],
                                              start=(h == 0), stop=(h == 1))
                mm.then_inc(lpw_done, 1)

            def salience(s):
                pe.wait_ge(abs_summed, s + 1)
                pe.wait_ge(newton_a, s)
                nc.tensor.matmul(PS[0:1, 7, 0:PT], ONES[:, 0:1], ADS[:], start=True, stop=True).then_inc(sal_ready, 1)

            def hidden(s, blocks=range(KH), with_a=True):
                if blocks[0] == 0:
                    pe.wait_ge(tconv_gelu, s + 1)
                    if with_a:
                        pe.wait_ge(ph_ready, 2 * s + 4)
                    pe.wait_ge(newton_a, s + 1)
                for m in blocks:
                    for h in range(2):
                        mm = nc.tensor.matmul(PS[:, (0, 1, 6)[m], 0:PT], W1P[:, h, 128 * m:128 * m + 128], TV[:, h, :],
                                              start=(h == 0), stop=(h == 1))
                    mm.then_inc(w1_done, 1)

            def transition(s):
                pe.wait_ge(local_out, s + 1)
                for k in range(KH):
                    pe.wait_ge(h_ready, KH * s + (KH + k + 1))
                    for m in range(2):
                        mm = nc.tensor.matmul(PS[0:HA, 2 + m, 0:PT], W2[:, k, HA * m:HA * m + HA], H1[:, k, :],
                                              start=(k == 0), stop=(k == KH - 1))
                mm.then_inc(w2_done, 1)

            def stats(s, with_a=True):
                for n in range(2):
                    pe.wait_ge(sq_summed, 2 * s + (n + 2))
                    if n and with_a:
                        pe.wait_ge(topk_step, 5 * s + 10)
                    mm = nc.tensor.matmul(PS[0:HA, 6 + n, 0:PT], ONES[:, 0:HA], SQS[:, n, :], start=True, stop=True)
                mm.then_inc(stats_done, 1)

            def up_block(k, m):
                pe.wait_ge(resid, KC * k + (m + 1))
                for h in range(2):
                    mm = nc.tensor.matmul(PS[:, 4 + m % 2, 0:PT], UP[:, h, 128 * m:128 * m + 128],
                                          FU[:, k & 1, h, :], start=(h == 0), stop=(h == 1))
                mm.then_inc(up_done, 1)

            def up(k, s=None):
                pe.wait_ge(scattered, k + 2)
                for m in range(KC):
                    up_block(k, m)
                    if s is not None and m == 1:
                        salience(s)

            def heads(c):
                pe.wait_ge(resid, KC * PAIRS * c + 2)
                pe.wait_ge(chain_dve, after("dve", c, "tok"))
                for part in range(2):
                    for hd in range(HEADS):
                        col = part * A + hd * DH
                        for h in range(2):
                            mm = nc.tensor.matmul(PS[0:DH, 4 + part, hd * NANC:(hd + 1) * NANC], AIN[:, h, col:col + DH],
                                                  TOK[:, h, :], start=(h == 0), stop=(h == 1))
                mm.then_inc(chain_pe, 1)

            def values(c):
                pe.wait_ge(chain_dve, after("dve", c, "q"))
                for h in range(2):
                    mm = nc.tensor.matmul(PS[:, 4, 0:A], TOK[:, h, :], AIN[:, h, 2 * A:3 * A], start=(h == 0), stop=(h == 1))
                mm.then_inc(chain_pe, 1)

            def scores(c):
                pe.wait_ge(chain_dve, after("dve", c, "k"))
                for hd in range(HEADS):
                    mm = nc.tensor.matmul(PS[:, 5, hd * NANC:(hd + 1) * NANC], QH[:, hd, :], KHD[:, hd, :], start=True, stop=True)
                mm.then_inc(chain_pe, 1)

            def turn(c):
                pe.wait_ge(chain_act, after("act", c, "v"))
                pe.wait_ge(chain_dve, after("dve", c, "prob"))
                for hd in range(HEADS):
                    mm = nc.tensor.transpose(PS[:, 4, hd * NANC:(hd + 1) * NANC], S[:, hd, :], IDENT)
                mm.then_inc(chain_pe, 1)

            def mix(c):
                pe.wait_ge(chain_dve, after("dve", c, "turned"))
                for hd in range(HEADS):
                    mm = nc.tensor.matmul(PS[0:DH, 5, hd * NANC:(hd + 1) * NANC], VV[:, hd * DH:(hd + 1) * DH], ST[:, hd, :],
                                          start=True, stop=True)
                mm.then_inc(chain_pe, 1)

            def attn_out(c):
                pe.wait_ge(chain_dve, after("dve", c, "mixed"))
                for m in range(2):
                    for hd in range(HEADS):
                        mm = nc.tensor.matmul(PS[0:HA, 4, m * NANC:(m + 1) * NANC], AOUT[:, hd, HA * m:HA * m + HA],
                                              OH[:, hd, :], start=(hd == 0), stop=(hd == HEADS - 1))
                mm.then_inc(chain_pe, 1)

            def anchors(c):
                pe.wait_ge(chain_dve, after("dve", c, "out"))
                for m in range(2):
                    for h in range(2):
                        mm = nc.tensor.matmul(PS[0:HA, 5, m * NANC:(m + 1) * NANC], APR[:, h, HA * m:HA * m + HA],
                                              A1[:, h, :], start=(h == 0), stop=(h == 1))
                mm.then_inc(chain_pe, 1)

            def mean_gate1(c):
                pe.wait_ge(chain_dve, after("dve", c, "ap_scaled"))
                for h in range(2):
                    nc.tensor.matmul(PS[0:HA, 4, 0:NANC], ONES[:, 0:HA], A2[:, h, :], start=(h == 0), stop=(h == 1))
                for m in range(2):
                    for q in range(4):
                        mm = nc.tensor.matmul(PS[0:HA, 4, 256 + m:257 + m], GW1[:, q, HA * m:HA * m + HA],
                                              GIN[:, q:q + 1], start=(q == 0), stop=(q == 3))
                mm.then_inc(chain_pe, 1)

            def anchor_var(c):
                pe.wait_ge(chain_act, after("act", c, "square"))
                for h in range(2):
                    mm = nc.tensor.matmul(PS[0:HA, 5, 0:NANC], ONES[:, 0:HA], ASQ[:, h, :], start=(h == 0), stop=(h == 1))
                mm.then_inc(chain_pe, 1)

            def gate2(c):
                pe.wait_ge(chain_act, after("act", c, "gelu"))
                for q in range(6):
                    for h in range(2):
                        mm = nc.tensor.matmul(PS[0:HA, 4, 300 + q:301 + q], GW2[:, h, HA * q:HA * q + HA], GH[:, h:h + 1],
                                              start=(h == 0), stop=(h == 1))
                mm.then_inc(chain_pe, 1)

            down(0)
            salience(0)
            down(1)
            local(0)
            salience(1)
            hidden(0)
            transition(0)
            with pe.Fori(2, PAIRS) as j:
                down(j)
                stats(j - 2)
                local(j - 1)
                salience(j)
                hidden(j - 1)
                transition(j - 1)
            with pe.Fori(1, B) as b:
                s, c = b * PAIRS, b - 1
                heads(c)
                down_start(s)
                down_blocks(s, (0, 1))
                values(c)
                scores(c)
                down_blocks(s, (2, 3, 4, 5))
                turn(c)
                stats(s - 2)
                mix(c)
                local(s - 1)
                attn_out(c)
                salience(s)
                hidden(s - 1, (0,))
                anchors(c)
                hidden(s - 1, (1, 2))
                mean_gate1(c)
                transition(s - 1)
                anchor_var(c)
                gate2(c)
                with pe.Fori(1, PAIRS) as j:
                    s = b * PAIRS + j
                    down(s)
                    stats(s - 2)
                    local(s - 1)
                    up(s - (PAIRS + 1), s)
                    hidden(s - 1)
                    transition(s - 1)
                up(b * PAIRS - 1)
            s, c = NPAIR - 1, B - 1
            heads(c)
            values(c)
            scores(c)
            stats(s - 1, False)
            local(s)
            turn(c)
            mix(c)
            hidden(s, (0, 1, 2), False)
            attn_out(c)
            transition(s)
            anchors(c)
            mean_gate1(c)
            stats(s, False)
            anchor_var(c)
            gate2(c)
            with pe.Fori(NPAIR - PAIRS, NPAIR) as k:
                up(k)
            pe.wait_ge(cls_loaded, 32)
            pe.wait_ge(cls_mean, 1)
            WC = XC[0:HA].rearrange("p k n -> p (k n)")[:, 0:2 * C].rearrange("p (h n) -> p h n", h=2)
            for m in range(KC):
                pe.wait_ge(resid, KC * NPAIR + 2)
                if m >= 2:
                    pe.wait_ge(cls_out, m - 1)
                for h in range(2):
                    mm = nc.tensor.matmul(PS[:, 4 + m % 2, 0:B * T], WC[:, h, 128 * m:128 * m + 128], FS[:, h, :],
                                          start=(h == 0), stop=(h == 1))
                mm.then_inc(cls_mm, 1)

        @block.scalar
        def _(act):
            act.sem_inc(h_ready, KH)
            act.sem_inc(trans_out, 1)
            act.wait_ge(setup_pe, 2)
            act.wait_ge(consts_set, 4)
            nc.scalar.activation(W1P[:], PS[0:HA, 0:2, 0:HID], ACT.Identity).then_inc(setup_act, 1)
            act.wait_ge(setup_dve, 7)

            def take_ph(s, j):
                act.wait_ge(xa_used, 2 * s + 4)
                act.wait_ge(gathered, s)
                hold(act, delta_ready, 2 * s)
                for h in range(2):
                    nc.scalar.activation(window(PH, h, ph_base(j & 1)),
                                         PS[0:HA, h, 0:PT].rearrange("p (f r c) -> p f r c", f=2, c=SIDE),
                                         ACT.Identity, bias=vec("down_b")[:, h:h + 1]).then_inc(ph_ready, 1)

            def take_abs(s, b, j):
                act.wait_ge(delta_ready, 2 * s + 2)
                hold(act, abs_summed, s)
                for h in range(2):
                    nc.scalar.activation(AD[:, h, :], DL[:, h, ds(2 * j + 1, 2), :].rearrange("p f n -> p (f n)"), ACT.Abs,
                                         accum_out=DPS[:, h, b & 1, ds(j, 1)]).then_inc(abs_ready, 1)

            def take_local(s, j):
                act.wait_ge(lpw_done, s + 1)
                hold(act, fused, s + 1)
                nc.scalar.activation(NRM[:, 0:2, j, :], halves(2), ACT.Identity).then_inc(local_out, 1)
                act.wait_ge(local_out, s + 1)
                hold(act, sq_summed, 2 * s + 1)
                nc.scalar.activation(SQ[:], NRM[:, 0:2, j, :], ACT.Square).then_inc(sq_ready, 1)

            def gelus(s):
                act.wait_ge(tconv_taps, 6 * s + 6)
                nc.scalar.activation(TV[:], TV[:], ACT.Gelu).then_inc(tconv_gelu, 1)
                act.wait_ge(w2_done, s + 1)
                for m in range(KH):
                    act.wait_ge(w1_done, KH * s + (m + 2))
                    nc.scalar.activation(H1[:, m, :], PS[:, (0, 1, 6)[m], 0:PT], ACT.Gelu,
                                         bias=VP[:, m:m + 1]).then_inc(h_ready, 1)

            def take_transition(s, j):
                hold(act, w2_done, s + 2)
                for h in range(2):
                    nc.scalar.activation(NRM[:, 2 + h, j, :], PS[0:HA, 2 + h, 0:PT], ACT.Identity,
                                         bias=vec("mlp_b2")[:, h:h + 1]).then_inc(trans_out, 1)
                act.wait_ge(trans_out, 2 * s + 3)
                hold(act, sq_summed, 2 * s + 2)
                nc.scalar.activation(SQ[:], NRM[:, 2:4, j, :], ACT.Square).then_inc(sq_ready, 1)

            def conv_gelus(s):
                act.wait_ge(conv_taps, 18 * s + 18)
                act.wait_ge(lpw_done, s)
                for h in range(2):
                    nc.scalar.activation(GL[:, h, :].rearrange("p (f r c) -> p f r c", f=2, c=SIDE),
                                         window(CV, h, 0), ACT.Gelu).then_inc(conv_gelu, 1)

            def rsqrts(s):
                act.wait_ge(stats_done, s + 2)
                act.wait_ge(normed, s + 1)
                nc.scalar.activation(RY[:], halves(6), ACT.Abs_reciprocal_sqrt, bias=EPSC[:]).then_inc(rs_first, 1)
                act.wait_ge(rs_first, s + 1)
                nc.scalar.activation(RT[:], RY[:], ACT.Square).then_inc(rs_square, 1)

            def take_values(c):
                act.wait_ge(chain_pe, after("pe", c, "v"))
                nc.scalar.activation(VV[:], PS[:, 4, 0:A], ACT.Identity).then_inc(chain_act, 1)

            def attn_exp(c):
                act.wait_ge(chain_dve, after("dve", c, "shifted"))
                nc.scalar.activation(S[:], S[:], ACT.Exp).then_inc(chain_act, 1)

            def anchor_squares(c):
                act.wait_ge(chain_dve, after("dve", c, "centred"))
                nc.scalar.activation(ASQ[:], XCN[:], ACT.Square).then_inc(chain_act, 1)

            def gate_gelu(c):
                act.wait_ge(chain_dve, after("dve", c, "gate1"))
                nc.scalar.activation(GH[:], GH[:], ACT.Gelu).then_inc(chain_act, 1)

            def gate_exp(c):
                act.wait_ge(chain_dve, after("dve", c, "gshift"))
                nc.scalar.activation(GT[:], GT[:], ACT.Exp).then_inc(chain_act, 1)

            def anchor_rsqrt(c):
                act.wait_ge(chain_pe, after("pe", c, "var"))
                nc.scalar.activation(AY[:], PS[0:HA, 5, 0:NANC], ACT.Abs_reciprocal_sqrt, bias=EPSC[:]).then_inc(chain_act, 1)
                act.wait_ge(chain_act, after("act", c, "rsqrt"))
                nc.scalar.activation(AT[:], AY[:], ACT.Square).then_inc(chain_act, 1)

            take_ph(0, 0)
            take_abs(0, 0, 0)
            conv_gelus(0)
            take_ph(1, 1)
            take_abs(1, 0, 1)
            take_local(0, 0)
            gelus(0)
            take_transition(0, 0)
            conv_gelus(1)
            with act.Fori(2, PAIRS) as j:
                take_ph(j, j)
                rsqrts(j - 2)
                take_abs(j, 0, j)
                take_local(j - 1, j - 1)
                gelus(j - 1)
                take_transition(j - 1, j - 1)
                conv_gelus(j)
            with act.Fori(1, B) as b:
                s, c = b * PAIRS, b - 1
                take_values(c)
                attn_exp(c)
                take_ph(s, 0)
                rsqrts(s - 2)
                take_abs(s, b, 0)
                take_local(s - 1, PAIRS - 1)
                gelus(s - 1)
                anchor_squares(c)
                gate_gelu(c)
                take_transition(s - 1, PAIRS - 1)
                conv_gelus(s)
                gate_exp(c)
                anchor_rsqrt(c)
                with act.Fori(1, PAIRS) as j:
                    s = b * PAIRS + j
                    take_ph(s, j)
                    rsqrts(s - 2)
                    take_abs(s, b, j)
                    take_local(s - 1, j - 1)
                    gelus(s - 1)
                    take_transition(s - 1, j - 1)
                    conv_gelus(s)
            s, c = NPAIR - 1, B - 1
            take_values(c)
            attn_exp(c)
            rsqrts(s - 1)
            take_local(s, PAIRS - 1)
            gelus(s)
            take_transition(s, PAIRS - 1)
            anchor_squares(c)
            gate_gelu(c)
            rsqrts(s)
            gate_exp(c)
            anchor_rsqrt(c)

        @block.gpsimd
        def _(pool):
            pool.memset(PH[:], 0.0).then_inc(consts_set, 1)
            pool.memset(DL[:, :, 0, :], 0.0).then_inc(consts_set, 1)
            pool.memset(DL[:, :, T + 1, :], 0.0).then_inc(consts_set, 1)
            for done in (gathered, sq_summed, scattered):
                pool.sem_inc(done, 1)
            pool.wait_ge(consts_set, 4)

            def sum_abs(s):
                pool.wait_ge(abs_ready, 2 * s + 2)
                pool.wait_ge(sal_ready, s)
                nc.gpsimd.tensor_tensor(ADS[:], AD[:, 0, :], AD[:, 1, :], ALU.add).then_inc(abs_summed, 1)

            def sum_squares(s, n):
                pool.wait_ge(sq_ready, 2 * s + (n + 1))
                pool.wait_ge(stats_done, s + 1)
                nc.gpsimd.tensor_tensor(SQS[:, n, :], SQ[:, 0, :], SQ[:, 1, :], ALU.add).then_inc(sq_summed, 1)

            def tokens(k):
                for f in range(2):
                    yield f, nc.values_load_multi_w_load_instructions(
                        IDX[0:1, k & (2 * PAIRS - 1), f * TOPK:(f + 1) * TOPK], engines=[pool.engine],
                        min_val=0, max_val=HW - 1)[1]

            def gather(s, b, j):
                pool.wait_ge(topk_step, 5 * s + 5)
                for f, frame in tokens(s):
                    for r, token in enumerate(frame):
                        last = nc.gpsimd.tensor_copy(G[:, b & 1, :, ds((2 * j + f) * TOPK + r, 1)],
                                                     PD[:, s & 1, :, ds(token + f * HW, 1)])
                last.then_inc(gathered, 1)

            def scatter(k, j):
                pool.wait_ge(fused, k + (PAIRS + 1))
                for f, frame in tokens(k):
                    for r, token in enumerate(frame):
                        at = FU[:, k & 1, :, ds(token + f * HW, 1)]
                        last = nc.gpsimd.tensor_tensor(at, at, Z[:, :, ds((2 * j + f) * TOPK + r, 1)], ALU.add)
                last.then_inc(scattered, 1)

            sum_abs(0)
            gather(0, 0, 0)
            with pool.Fori(1, PAIRS) as j:
                sum_abs(j)
                sum_squares(j - 1, 0)
                gather(j, 0, j)
                sum_squares(j - 1, 1)
            with pool.Fori(1, B) as b:
                s = b * PAIRS
                sum_abs(s)
                sum_squares(s - 1, 0)
                gather(s, b, 0)
                sum_squares(s - 1, 1)
                scatter(s - PAIRS, 0)
                with pool.Fori(1, PAIRS) as j:
                    s = b * PAIRS + j
                    sum_abs(s)
                    sum_squares(s - 1, 0)
                    gather(s, b, j)
                    sum_squares(s - 1, 1)
                    scatter(s - PAIRS, j)
            sum_squares(NPAIR - 1, 0)
            sum_squares(NPAIR - 1, 1)
            with pool.Fori(0, PAIRS) as j:
                scatter(NPAIR - PAIRS + j, j)

        @block.vector
        def _(dve):
            v = nc.vector
            dve.sem_inc(newton_a, 1)
            dve.sem_inc(normed, 1)
            dve.sem_inc(fused, PAIRS)
            dve.sem_inc(resid, 2)
            dve.sem_inc(up_done, 2 * KC)
            v.memset(EPSC[:], EPS)
            v.memset(ONES[:], 1.0 / A).then_inc(consts_set, 1)
            dve.wait_ge(consts_set, 4)
            dve.wait_ge(wts_loaded, 16 * (WEIGHT_LOADS - 1))
            v.tensor_reduce(WM[0:HA, 0:2], LPW, AX.X, ALU.add)
            v.tensor_reduce(WM[:, 2:2 + KH], W2[:], AX.X, ALU.add).then_inc(setup_dve, 1)
            dve.wait_ge(setup_dve, 1)
            v.tensor_scalar(WM[:, 2:2 + KH], WM[:, 2:2 + KH], 1.0 / A, None, ALU.mult).then_inc(setup_dve, 1)
            v.tensor_scalar(WM[0:HA, 0:2], WM[0:HA, 0:2], 1.0 / A, None, ALU.mult).then_inc(setup_dve, 1)
            dve.wait_ge(setup_dve, 3)
            for h in range(2):
                v.tensor_scalar(LPW[:, h, :], LPW[:, h, :], WM[0:HA, h:h + 1], None, ALU.subtract)
            for k in range(KH):
                v.tensor_scalar(W2[:, k, :], W2[:, k, :], WM[:, 2 + k:3 + k], None, ALU.subtract).then_inc(setup_dve, 1)
            dve.wait_ge(setup_pe, 3)
            v.tensor_tensor(vec("mlp_b2"), vec("mlp_b2"), PS[0:HA, 2, 0:1].to_broadcast([HA, 2]), ALU.subtract).then_inc(setup_dve, 1)

            def delta(s, b, j):
                dve.wait_ge(ph_ready, 2 * s + 2)
                here = ph_base(j & 1)
                before = here if isinstance(j, int) and j == 0 else ph_base(1 - (j & 1)) + FP
                for f, prev in ((0, before), (1, here)):
                    v.tensor_tensor(DL[:, :, ds(2 * j + 1 + f, 1), :].rearrange("p h f (r c) -> p h (f r) c", c=SIDE),
                                    frame2(PH, here + f * FP), frame2(PH, prev), ALU.subtract).then_inc(delta_ready, 1)

            def anchor_source(s, j):
                dve.wait_ge(gathered, s)
                for f in range(2):
                    dve.wait_ge(delta_ready, 2 * s + (f + 1))
                    v.tensor_tensor(PD[:, s & 1, :, f * HW:(f + 1) * HW].rearrange("p h (r c) -> p h r c", c=SIDE),
                                    frame2(PH, ph_base(j & 1) + f * FP),
                                    DL[:, :, ds(2 * j + 1 + f, 1), :].rearrange("p h f (r c) -> p h (f r) c", c=SIDE),
                                    ALU.add).then_inc(ph_delta, 1)

            def tconv(s, j, with_a=True):
                dve.wait_ge(w1_done, KH * s + 1)
                dve.wait_ge(delta_ready, 2 * s + (4 if with_a else 2))
                for k in range(3):
                    for h in range(2):
                        src = DL[:, h, ds(2 * j + k, 2), :].rearrange("p f n -> p (f n)")
                        if k == 0:
                            tap = v.tensor_scalar(TV[:, h, :], src, TDW[:, h, 0:1], None, ALU.mult)
                        else:
                            dve.wait_ge(tconv_taps, 6 * s + (2 * k + h - 1))
                            tap = v.scalar_tensor_tensor(out=TV[:, h, :], in0=src, scalar=TDW[:, h, k:k + 1],
                                                         in1=TV[:, h, :], op0=ALU.mult, op1=ALU.add)
                        tap.then_inc(tconv_taps, 1)

            def conv_taps_of(s, j, first, last):
                for step in range(first, last):
                    k, h = step // 2, step % 2
                    src = rows(PH, h, ph_base(j & 1) + (k // 3 - 1) * PITCH + (k % 3 - 1))
                    dst = rows(CV, h, 0)
                    if k == 0:
                        if h == 0:
                            dve.wait_ge(conv_gelu, 2 * s)
                        tap = v.tensor_scalar(dst, src, LDW[:, h, 0:1], None, ALU.mult)
                    else:
                        dve.wait_ge(conv_taps, 18 * s + (step - 1))
                        tap = v.scalar_tensor_tensor(out=dst, in0=src, scalar=LDW[:, h, k:k + 1], in1=dst,
                                                     op0=ALU.mult, op1=ALU.add)
                    tap.then_inc(conv_taps, 1)

            def frame_sums(k):
                dve.wait_ge(scattered, k + 2)
                v.tensor_reduce(FS[:, :, ds(2 * k, 2)], FU[:, k & 1, :, :].rearrange("p h (f n) -> p h f n", f=2), AX.X, ALU.add)

            def residual(k, m):
                dve.wait_ge(up_done, KC * k + (m + 1 + 2 * KC))
                if m % HK == 0:
                    dve.wait_ge(xc_loaded[m // HK], 16 * k + 16)
                v.scalar_tensor_tensor(out=XC[:, m, :], in0=PS[:, 4 + m % 2, 0:PT], scalar=VP[:, KH + m:KH + m + 1],
                                       in1=XC[:, m, :], op0=ALU.add, op1=ALU.add).then_inc(resid, 1)

            def topk(s):
                hold(dve, sal_ready, s + 1)
                for f in range(2):
                    sal = PS[0:1, 7, f * HW:(f + 1) * HW]
                    v.max(MX[:, f, :], sal).then_inc(topk_step, 1)
                for f in range(2):
                    sal = PS[0:1, 7, f * HW:(f + 1) * HW]
                    hold(dve, topk_step, 5 * s + 2)
                    v.max_index(IDN[:, f * TOPK:(f + 1) * TOPK], MX[:, f, :], sal).then_inc(topk_step, 1)
                dve.wait_ge(topk_step, 5 * s + 4)
                v.tensor_copy(IDX[0:1, s & (2 * PAIRS - 1), :], IDN[:]).then_inc(topk_step, 1)

            def fuse(k, j):
                dve.wait_ge(up_done, KC * k + KC)
                dve.wait_ge(fused, k + PAIRS)
                for h in range(2):
                    v.tensor_scalar(FT[:, h, :], NRM[:, 2 + h, j, :], GG[:, 2 + h:3 + h], GC[:, h:h + 1],
                                    ALU.mult, ALU.add).then_inc(weighted, 1)
                for h in range(2):
                    dve.wait_ge(weighted, 2 * k + (h + 1))
                    last = v.scalar_tensor_tensor(out=FU[:, k & 1, h, :], in0=NRM[:, h, j, :], scalar=GG[:, h:h + 1],
                                                  in1=FT[:, h, :], op0=ALU.mult, op1=ALU.add)
                last.then_inc(fused, 1)

            def finalize(s, j):
                dve.wait_ge(rs_square, s + 1)
                v.scalar_tensor_tensor(out=RT[:], in0=halves(6), scalar=EPSC[:], in1=RT[:],
                                       op0=ALU.add, op1=ALU.mult).then_inc(newton_a, 1)
                dve.wait_ge(newton_a, s + 2)
                v.tensor_scalar(RT[:], RT[:], -0.5, 1.5, ALU.mult, ALU.add).then_inc(newton_b, 1)
                dve.wait_ge(newton_b, s + 1)
                v.tensor_tensor(RY[:], RY[:], RT[:], ALU.mult).then_inc(newton_c, 1)
                dve.wait_ge(newton_c, s + 1)
                for n in range(2):
                    last = v.tensor_tensor(NRM[:, 2 * n:2 * n + 2, j, :], NRM[:, 2 * n:2 * n + 2, j, :],
                                           RY[:, n:n + 1, :].to_broadcast([HA, 2, PT]), ALU.mult)
                last.then_inc(normed, 1)

            def link(instruction, c, step):
                instruction.then_inc(chain_dve, 1)
                dve.wait_ge(chain_dve, after("dve", c, step))

            def clip_delta(c):
                link(v.tensor_reduce(GIN[:, 0:2], DPS[:, :, c & 1, :], AX.X, ALU.add), c, "dp")
                link(v.tensor_scalar(GIN[:, 0:2], GIN[:, 0:2], 1.0 / (T * HW), None, ALU.mult), c, "dp_scaled")
                dve.wait_ge(gathered, PAIRS * c + (PAIRS + 1))
                link(v.tensor_copy(TOK[:], G[:, c & 1, :, :]), c, "tok")

            def take_heads(c):
                dve.wait_ge(chain_pe, after("pe", c, "qk"))
                for part, dst, step in ((0, QH, "q"), (1, KHD, "k")):
                    link(v.tensor_tensor(dst[:], PS[0:DH, 4 + part, 0:HEADS * NANC].rearrange("p (h n) -> p h n", h=HEADS),
                                         VH[:, part, :].unsqueeze(2).to_broadcast([DH, HEADS, NANC]), ALU.add), c, step)

            def softmax_top(c):
                dve.wait_ge(chain_pe, after("pe", c, "scores"))
                link(v.scalar_tensor_tensor(out=S[:], in0=PS[:, 5, 0:HEADS * NANC].rearrange("p (h n) -> p h n", h=HEADS),
                                            scalar=float(DH) ** -0.5,
                                            in1=MASK.unsqueeze(1).to_broadcast([NANC, HEADS, NANC]),
                                            op0=ALU.mult, op1=ALU.add), c, "masked")
                link(v.tensor_reduce(SM[:, 0, :], S[:], AX.X, ALU.max), c, "max")
                link(v.tensor_tensor(S[:], S[:], SM[:, 0, :].unsqueeze(2).to_broadcast([NANC, HEADS, NANC]),
                                     ALU.subtract), c, "shifted")

            def softmax_end(c):
                dve.wait_ge(chain_act, after("act", c, "exp"))
                link(v.tensor_reduce(SM[:, 1, :], S[:], AX.X, ALU.add), c, "sum")
                link(v.reciprocal(SM[:, 2, :], SM[:, 1, :]), c, "recip")
                link(v.tensor_tensor(S[:], S[:], SM[:, 2, :].unsqueeze(2).to_broadcast([NANC, HEADS, NANC]),
                                     ALU.mult), c, "prob")

            def take_turned(c):
                dve.wait_ge(chain_pe, after("pe", c, "turned"))
                link(v.tensor_copy(ST[:], PS[:, 4, 0:HEADS * NANC].rearrange("p (h n) -> p h n", h=HEADS)), c, "turned")

            def take_mixed(c):
                dve.wait_ge(chain_pe, after("pe", c, "mixed"))
                link(v.tensor_tensor(OH[:], PS[0:DH, 5, 0:HEADS * NANC].rearrange("p (h n) -> p h n", h=HEADS),
                                     VH[:, 2, :].unsqueeze(2).to_broadcast([DH, HEADS, NANC]), ALU.add), c, "mixed")

            def take_projected(c, bank, dst, bias, step):
                dve.wait_ge(chain_pe, after("pe", c, step))
                link(v.tensor_tensor(dst[:], PS[0:HA, bank, 0:2 * NANC].rearrange("p (h n) -> p h n", h=2),
                                     vec(bias).unsqueeze(2).to_broadcast([HA, 2, NANC]), ALU.add), c, step)

            def take_anchors(c):
                take_projected(c, 5, A2, "proj_b", "anchor")
                link(v.tensor_reduce(GIN[:, 2:4], A2[:], AX.X, ALU.add), c, "ap")
                link(v.tensor_scalar(GIN[:, 2:4], GIN[:, 2:4], 1.0 / NANC, None, ALU.mult), c, "ap_scaled")

            def centre(c):
                dve.wait_ge(chain_pe, after("pe", c, "mean_gate1"))
                link(v.tensor_tensor(XCN[:], A2[:], PS[0:HA, 4, 0:NANC].unsqueeze(1).to_broadcast([HA, 2, NANC]),
                                     ALU.subtract), c, "centred")
                link(v.tensor_tensor(GH[:], vec("gate_b1"), PS[0:HA, 4, 256:258], ALU.add), c, "gate1")

            three = [HA, 3, 2]
            g3 = GT[:].rearrange("p (g h) -> p g h", h=2)

            def gates_top(c):
                dve.wait_ge(chain_pe, after("pe", c, "gate2"))
                link(v.tensor_tensor(GT[:], vec("gate_b2"), PS[0:HA, 4, 300:306], ALU.add), c, "gate2")
                link(v.tensor_tensor(GM[:], GT[:, 0:2], GT[:, 2:4], ALU.max), c, "gmax1")
                link(v.tensor_tensor(GM[:], GM[:], GT[:, 4:6], ALU.max), c, "gmax2")
                link(v.tensor_tensor(g3, g3, GM[:].unsqueeze(1).to_broadcast(three), ALU.subtract), c, "gshift")

            def gates_end(c):
                dve.wait_ge(chain_act, after("act", c, "gate_exp"))
                link(v.tensor_tensor(GM[:], GT[:, 0:2], GT[:, 2:4], ALU.add), c, "gsum1")
                link(v.tensor_tensor(GM[:], GM[:], GT[:, 4:6], ALU.add), c, "gsum2")
                link(v.reciprocal(GM[:], GM[:]), c, "grecip")
                link(v.tensor_tensor(g3, g3, GM[:].unsqueeze(1).to_broadcast(three), ALU.mult), c, "gates")
                link(v.tensor_tensor(GG[:], GT[:], vec("gain"), ALU.mult), c, "gains")
                link(v.tensor_tensor(GB[:], GT[:], vec("beta"), ALU.mult), c, "betas")
                link(v.tensor_tensor(GC[:], GB[:, 0:2], GB[:, 2:4], ALU.add), c, "const1")
                link(v.tensor_tensor(GC[:], GC[:], GB[:, 4:6], ALU.add), c, "const2")

            def anchor_norm(c):
                dve.wait_ge(chain_act, after("act", c, "rsqrt_sq"))
                link(v.scalar_tensor_tensor(out=AT[:], in0=PS[0:HA, 5, 0:NANC], scalar=EPSC[:], in1=AT[:],
                                            op0=ALU.add, op1=ALU.mult), c, "newton1")
                link(v.tensor_scalar(AT[:], AT[:], -0.5, 1.5, ALU.mult, ALU.add), c, "newton2")
                link(v.tensor_tensor(AY[:], AY[:], AT[:], ALU.mult), c, "newton3")
                dve.wait_ge(scattered, PAIRS * c + 1)
                link(v.tensor_tensor(Z[:], XCN[:], AY[:].unsqueeze(1).to_broadcast([HA, 2, NANC]), ALU.mult), c, "znorm")
                link(v.tensor_tensor(Z[:], Z[:], GG[:, 4:6].unsqueeze(2).to_broadcast([HA, 2, NANC]), ALU.mult), c, "z")

            def front(s, b, j):
                delta(s, b, j)
                anchor_source(s, j)

            def finish(k):
                frame_sums(k)
                for m in range(KC):
                    residual(k, m)

            front(0, 0, 0)
            topk(0)
            conv_taps_of(0, 0, 0, 18)
            front(1, 0, 1)
            tconv(0, 0)
            topk(1)
            conv_taps_of(1, 1, 0, 18)
            with dve.Fori(2, PAIRS) as j:
                front(j, 0, j)
                tconv(j - 1, j - 1)
                finalize(j - 2, j - 2)
                topk(j)
                conv_taps_of(j, j, 0, 18)
            with dve.Fori(1, B) as b:
                s, c = b * PAIRS, b - 1
                clip_delta(c)
                take_heads(c)
                softmax_top(c)
                softmax_end(c)
                take_turned(c)
                front(s, b, 0)
                take_mixed(c)
                tconv(s - 1, PAIRS - 1)
                take_projected(c, 4, A1, "out_b", "out")
                finalize(s - 2, PAIRS - 2)
                take_anchors(c)
                topk(s)
                centre(c)
                conv_taps_of(s, 0, 0, 8)
                gates_top(c)
                conv_taps_of(s, 0, 8, 18)
                gates_end(c)
                anchor_norm(c)
                fuse(s - PAIRS, 0)
                with dve.Fori(1, PAIRS) as j:
                    s = b * PAIRS + j
                    k = s - (PAIRS + 1)
                    front(s, b, j)
                    tconv(s - 1, j - 1)
                    finalize(s - 2, (j + (PAIRS - 2)) & (PAIRS - 1))
                    frame_sums(k)
                    for m in range(KC):
                        residual(k, m)
                        conv_taps_of(s, j, m, m + 1)
                        if m == 3:
                            topk(s)
                    conv_taps_of(s, j, KC, 18)
                    fuse(s - PAIRS, j)
                finish(b * PAIRS - 1)
            s, c = NPAIR - 1, B - 1
            clip_delta(c)
            take_heads(c)
            softmax_top(c)
            softmax_end(c)
            finalize(s - 1, PAIRS - 2)
            take_turned(c)
            tconv(s, PAIRS - 1, False)
            take_mixed(c)
            take_projected(c, 4, A1, "out_b", "out")
            take_anchors(c)
            centre(c)
            finalize(s, PAIRS - 1)
            gates_top(c)
            gates_end(c)
            anchor_norm(c)
            fuse(NPAIR - PAIRS, 0)
            with dve.Fori(1, PAIRS) as j:
                fuse(NPAIR - PAIRS + j, j)
                finish(NPAIR - PAIRS - 1 + j)
            finish(NPAIR - 1)
            v.tensor_scalar(FS[:], FS[:], 1.0 / HW, None, ALU.mult).then_inc(cls_mean, 1)
            XK = XA[:].rearrange("p k n -> p (k n)")[:, 0:KC * B * T].rearrange("p (k n) -> p k n", k=KC)
            dve.wait_ge(cls_loaded, 32)
            for m in range(KC):
                dve.wait_ge(cls_mm, m + 1)
                v.scalar_tensor_tensor(out=XK[:, m, :], in0=PS[:, 4 + m % 2, 0:B * T],
                                       scalar=VP[:, KH + KC + m:KH + KC + m + 1], in1=XK[:, m, :],
                                       op0=ALU.add, op1=ALU.add).then_inc(cls_out, 1)


def kernel(**inputs):
    import numpy as np
    import concourse.bacc as bacc
    from concourse.bass_utils import run_bass_kernel_spmd

    a = {k.replace("L0_conv_", ""): np.asarray(v) for k, v in inputs.items()}
    x = a["x"]

    def by(n, w):
        k = w.shape[0] // n
        return w.reshape(k, n, *w.shape[1:]).swapaxes(0, 1)

    def flat(w):
        return w.reshape(w.shape[0], -1)

    vectors = {"down_b": by(HA, a["down_b"]), "mlp_b2": by(HA, a["tmlp_b2"]), "out_b": by(HA, a["attn_out_b"]),
               "gain": np.concatenate([by(HA, a[n]) for n in ("lnorm_g", "tnorm_g", "anorm_g")], 1),
               "beta": np.concatenate([by(HA, a[n]) for n in ("lnorm_b", "tnorm_b", "anorm_b")], 1),
               "proj_b": by(HA, a["aproj_b"]), "gate_b1": by(HA, a["gate_b1"]), "gate_b2": by(HA, a["gate_b2"]),
               "ldw": flat(by(HA, a["ldw_w"].reshape(A, 9))), "tdw": flat(by(HA, a["tdw_w"].reshape(A, 3)))}
    weights = {"lpw": a["lpw_w"], "up": a["up_w"], "attn_in": a["attn_in_w"], "aproj": a["aproj_w"],
               "gate1": a["gate_w1"], "gate2": a["gate_w2"]}
    place = np.arange(NANC)
    mask = np.where((place[:, None] - place[None, :]) % TOPK == 0, 0.0, -1e30)
    arrays = {
        "xp": x[:, :, 1:, :].reshape(B, PAIRS, 2, HW, KC, 128).transpose(0, 1, 5, 4, 2, 3).reshape(NPAIR, 128, KC, PT),
        "xcls": x[:, :, 0, :].reshape(B * T, KC, 128).transpose(2, 1, 0).reshape(128, KC * B * T),
        "wdown": by(128, a["down_w"].T),
        "w96": np.concatenate([flat(by(HA, weights[n].T)) for n in W96], 1),
        "wsetup": np.concatenate([flat(by(HA, a["tpw_w"])), flat(by(HA, a["tmlp_w1"].T))], 1),
        "wcls": flat(by(HA, a["cls_w"].T)),
        "w2": by(128, a["tmlp_w2"].T),
        "aout": by(DH, a["attn_out_w"].T),
        "v96": np.concatenate([vectors[n] for n in V96], 1),
        "v48": a["attn_in_b"].reshape(3, HEADS, DH).transpose(2, 0, 1),
        "v128": np.concatenate([by(128, a[n]) for n in ("tmlp_b1", "up_b", "cls_b")], 1),
        "consts": np.stack([np.eye(128), mask], 1).astype(np.float32),
    }
    arrays = {k: np.ascontiguousarray(v, dtype=np.float32) for k, v in arrays.items()}
    nc = bacc.Bacc("TRN2", target_bir_lowering=False, num_devices=1)
    args = [nc.dram_tensor(k, v.shape, F32, kind="ExternalInput").ap() for k, v in arrays.items()]
    args.append(nc.dram_tensor("out", (NPAIR, 128, KC, PT), F32, kind="ExternalOutput").ap())
    args.append(nc.dram_tensor("outcls", (128, KC * B * T), F32, kind="ExternalOutput").ap())
    build(nc, *args)
    r = run_bass_kernel_spmd(nc, [arrays], core_ids=[0]).results[0]
    patch = r["out"].reshape(B, PAIRS, 128, KC, 2, HW).transpose(0, 1, 4, 5, 3, 2).reshape(B, T, HW, C)
    cls = r["outcls"].reshape(128, KC, B * T).transpose(2, 1, 0).reshape(B, T, 1, C)
    return np.concatenate([cls, patch], 2)
```

```python
from contextlib import ExitStack

import concourse.bass as bass
from concourse import mybir

F32 = mybir.dt.float32
U32 = mybir.dt.uint32
ACT = mybir.ActivationFunctionType
ALU = mybir.AluOpType
AX = mybir.AxisListType

B, T, SIDE, C, A = 16, 16, 14, 768, 192
HW = SIDE * SIDE
PT = 2 * HW
HA = A // 2
KC = C // 128
PAIRS = T // 2
NPAIR = B * PAIRS
HID = 2 * A
KH = HID // 128
TOPK, HEADS = 8, 4
DH = A // HEADS
NANC = T * TOPK
EPS = 1e-5
PITCH = SIDE + 1
FP = PITCH * PITCH
GUARD = PITCH + 1
ROWS = 2 * SIDE + 1
SPAN = ROWS * PITCH

V96 = {}
_at = 0
for _name, _n in (("down_b", 2), ("gain", 6), ("beta", 6), ("mlp_b2", 2), ("out_b", 2), ("proj_b", 2),
                  ("gate_b1", 2), ("gate_b2", 6), ("ldw", 18), ("tdw", 6)):
    V96[_name] = (_at, _n)
    _at += _n
NV96 = _at
W96 = {}
_at = 0
for _name, _n in (("lpw", 2 * A), ("up", 2 * C), ("attn_in", 2 * 3 * A), ("aproj", 2 * A),
                  ("gate1", 4 * A), ("gate2", 2 * 3 * A)):
    W96[_name] = (_at, _n)
    _at += _n
NW96 = _at
NSETUP = 2 * A + 2 * HID

CHAIN = {
    "pe": ["qk", "v", "scores", "turned", "mixed", "out", "anchor", "mean_gate1", "gate2", "var"],
    "act": ["v", "exp", "square", "gelu", "gate_exp", "rsqrt", "rsqrt_sq"],
    "dve": ["dp", "dp_scaled", "tok", "q", "k", "masked", "max", "shifted", "sum", "recip", "prob",
            "turned", "mixed", "out", "anchor", "ap", "ap_scaled", "centred", "gate1", "gate2",
            "gmax1", "gmax2", "gshift", "gsum1", "gsum2", "grecip", "gates", "gains", "betas",
            "const1", "const2", "newton1", "newton2", "newton3", "znorm", "z"],
}


def after(engine, clip, step):
    steps = CHAIN[engine]
    return clip * len(steps) + (steps.index(step) + 1)


def build(nc, xp, xcls, wdown, w96, wsetup, wcls, w2, aout, v96, v48, v128, consts, out, outcls):
    ds = bass.ds
    with ExitStack() as ctx:
        def sb(name, shape, dt=F32):
            return ctx.enter_context(nc.sbuf_tensor(name, shape, dt))

        def sem(name):
            return ctx.enter_context(nc.semaphore(name))

        WD = sb("WD", [128, KC, A])
        W = sb("W", [HA, NW96])
        W1P = sb("W1P", [HA, 2, HID])
        W2 = sb("W2", [128, KH, A])
        AOUT = sb("AOUT", [DH, HEADS, A])
        VA = sb("VA", [HA, NV96])
        VH = sb("VH", [DH, 3, HEADS])
        VP = sb("VP", [128, KH + 2 * KC])
        CST = sb("CST", [128, 2, 128])
        ONES = sb("ONES", [HA, 128])
        EPSC = sb("EPSC", [HA, 1])
        WARM = sb("WARM", [HA, 1])
        WM = sb("WM", [128, 8])

        def wt(name, n):
            a, m = W96[name]
            return W[:, a:a + m].rearrange("p (k n) -> p k n", n=n)

        def vec(name):
            a, m = V96[name]
            return VA[:, a:a + m]

        LPW, UP, AIN = wt("lpw", A), wt("up", C), wt("attn_in", 3 * A)
        APR, GW1, GW2 = wt("aproj", A), wt("gate1", A), wt("gate2", 3 * A)
        LDW = vec("ldw").rearrange("p (h k) -> p h k", k=9)
        TDW = vec("tdw").rearrange("p (h k) -> p h k", k=3)
        IDENT, MASK = CST[:, 0, :], CST[:, 1, :]

        XA = sb("XA", [128, KC, PT])
        XC = sb("XC", [128, KC, PT])
        PH = sb("PH", [HA, 2, GUARD + 4 * FP + 2])
        DL = sb("DL", [HA, 2, T + 2, HW])
        NRM = sb("NRM", [HA, 4, PAIRS, PT])
        CV = sb("CV", [HA, 2, 2 * FP])
        TV = sb("TV", [HA, 2, PT])
        GL = sb("GL", [HA, 2, PT])
        H1 = sb("H1", [128, KH, PT])
        AD = sb("AD", [HA, 2, PT])
        PD = sb("PD", [HA, 2, 2, PT])
        ADS = sb("ADS", [HA, PT])
        SQ = sb("SQ", [HA, 2, PT])
        SQS = sb("SQS", [HA, 2, PT])
        RY = sb("RY", [HA, 2, PT])
        RT = sb("RT", [HA, 2, PT])
        FT = sb("FT", [HA, 2, PT])
        FU = sb("FU", [HA, 2, 2, PT])
        FS = sb("FS", [HA, 2, B * T])
        MX = sb("MX", [1, 2, TOPK])
        IDN = sb("IDN", [1, 2 * TOPK], U32)
        IDX = sb("IDX", [1, 2 * PAIRS, 2 * TOPK], U32)
        DPS = sb("DPS", [HA, 2, 2, PAIRS])
        G = sb("G", [HA, 2, 2, NANC])
        TOK = sb("TOK", [HA, 2, NANC])
        QH = sb("QH", [DH, HEADS, NANC])
        KHD = sb("KHD", [DH, HEADS, NANC])
        VV = sb("VV", [NANC, A])
        S = sb("S", [NANC, HEADS, NANC])
        ST = sb("ST", [NANC, HEADS, NANC])
        SM = sb("SM", [NANC, 3, HEADS])
        OH = sb("OH", [DH, HEADS, NANC])
        A1 = sb("A1", [HA, 2, NANC])
        A2 = sb("A2", [HA, 2, NANC])
        XCN = sb("XCN", [HA, 2, NANC])
        ASQ = sb("ASQ", [HA, 2, NANC])
        AY = sb("AY", [HA, NANC])
        AT = sb("AT", [HA, NANC])
        Z = sb("Z", [HA, 2, NANC])
        GIN = sb("GIN", [HA, 4])
        GH = sb("GH", [HA, 2])
        GT = sb("GT", [HA, 6])
        GM = sb("GM", [HA, 2])
        GG = sb("GG", [HA, 6])
        GB = sb("GB", [HA, 6])
        GC = sb("GC", [HA, 2])

        PS = ctx.enter_context(nc.psum_tensor("PS", [128, 8, 512], F32))

        wts_loaded = sem("wts_loaded")
        consts_set = sem("consts_set")
        holds = sem("holds")
        setup_pe = sem("setup_pe")
        setup_dve = sem("setup_dve")
        setup_act = sem("setup_act")
        xa_loaded = [sem(f"xa_loaded{h}") for h in range(2)]
        xc_loaded = [sem(f"xc_loaded{h}") for h in range(2)]
        stored = [sem(f"stored{h}") for h in range(2)]
        stored_xa = [sem(f"stored_xa{h}") for h in range(2)]
        xa_used = sem("xa_used")
        ph_ready = sem("ph_ready")
        delta_ready = sem("delta_ready")
        ph_delta = sem("ph_delta")
        abs_ready = sem("abs_ready")
        abs_summed = sem("abs_summed")
        sal_ready = sem("sal_ready")
        topk_step = sem("topk_step")
        gathered = sem("gathered")
        conv_taps = sem("conv_taps")
        conv_gelu = sem("conv_gelu")
        tconv_taps = sem("tconv_taps")
        tconv_gelu = sem("tconv_gelu")
        lpw_done = sem("lpw_done")
        local_out = sem("local_out")
        sq_ready = sem("sq_ready")
        sq_summed = sem("sq_summed")
        w1_done = sem("w1_done")
        h_ready = sem("h_ready")
        w2_done = sem("w2_done")
        trans_out = sem("trans_out")
        stats_done = sem("stats_done")
        rs_first = sem("rs_first")
        rs_square = sem("rs_square")
        newton_a = sem("newton_a")
        newton_b = sem("newton_b")
        newton_c = sem("newton_c")
        normed = sem("normed")
        normed_trans = sem("normed_trans")
        weighted = sem("weighted")
        fused = sem("fused")
        scattered = sem("scattered")
        frames_summed = sem("frames_summed")
        up_done = sem("up_done")
        resid = sem("resid")
        chain_pe = sem("chain_pe")
        chain_act = sem("chain_act")
        chain_dve = sem("chain_dve")
        cls_loaded = sem("cls_loaded")
        cls_mean = sem("cls_mean")
        cls_mm = sem("cls_mm")
        cls_out = sem("cls_out")
        cls_stored = sem("cls_stored")

        block = ctx.enter_context(nc.Block())

        WEIGHT_LOADS = 10

        def hold(eng, semaphore, value):
            eng.wait_ge(semaphore, value)
            eng.sem_inc(holds, 1)

        HK = KC // 2

        def halves(bank, n=PT, p=HA):
            return PS[0:p, bank:bank + 2, 0:n]

        def ph_base(slot):
            return GUARD + slot * (2 * FP)

        def window(tile, half, start, frames=2):
            v = tile[:, half, ds(start, frames * FP)]
            return v.rearrange("p (f r c) -> p f r c", r=PITCH, c=PITCH)[:, :, 0:SIDE, 0:SIDE]

        def frame2(tile, start):
            v = tile[:, :, ds(start, FP)]
            return v.rearrange("p h (r c) -> p h r c", c=PITCH)[:, :, 0:SIDE, 0:SIDE]

        def rows(tile, half, start):
            v = tile[:, half, ds(start, SPAN)]
            return v.rearrange("p (r c) -> p r c", c=PITCH)[:, :, 0:SIDE]

        @block.sync
        def _(sp):
            for h in range(2):
                sp.sem_inc(stored[h], 16)
                sp.sem_inc(stored_xa[h], 16)
            for dst, src in ((WD[:], wdown), (W[:], w96), (XC[0:HA].rearrange("p k n -> p (k n)")[:, 0:NSETUP], wsetup),
                             (W2[:], w2), (AOUT[:], aout), (VA[:], v96), (VH[:], v48), (VP[:], v128),
                             (CST[:], consts)):
                sp.dma_start(dst, src).then_inc(wts_loaded, 16)

            def load_xa(s):
                for h in range(2):
                    sp.wait_ge(xa_used, 2 * s + (h + 1))
                    sp.dma_start(XA[:, HK * h:HK * h + HK, :], xp[s, :, HK * h:HK * h + HK, :]).then_inc(xa_loaded[h], 16)

            def load_xc(k, former=None):
                former = k if former is None else former
                for h in range(2):
                    sp.wait_ge(stored[h], 16 * former + 16)
                    sp.dma_start(XC[:, HK * h:HK * h + HK, :], xp[k, :, HK * h:HK * h + HK, :]).then_inc(xc_loaded[h], 16)

            def store(k, buffer=XC, signal=stored):
                for h in range(2):
                    sp.wait_ge(resid, KC * k + (HK * (h + 1) + 2))
                    sp.dma_start(out[k, :, HK * h:HK * h + HK, :], buffer[:, HK * h:HK * h + HK, :]).then_inc(signal[h], 16)

            AHEAD = PAIRS + 2
            for s in range(AHEAD):
                load_xa(s)
                if s == 1:
                    sp.wait_ge(setup_pe, 2)
                    load_xc(0)
            with sp.Fori(0, NPAIR - AHEAD) as k:
                load_xa(k + AHEAD)
                store(k)
                load_xc(k + 1)
            store(NPAIR - AHEAD)
            load_xc(NPAIR - AHEAD + 1)
            FIRST = NPAIR - PAIRS

            def reload_xa(pair):
                for h in range(2):
                    sp.wait_ge(stored_xa[h], 8 * pair + 16)
                    sp.dma_start(XA[:, HK * h:HK * h + HK, :],
                                 xp[FIRST + pair, :, HK * h:HK * h + HK, :]).then_inc(xa_loaded[h], 16)

            sp.wait_ge(xa_used, 2 * NPAIR + 2)
            reload_xa(0)
            store(FIRST - 1)
            load_xc(FIRST + 1, FIRST)
            sp.wait_ge(tconv_taps, 6 * NPAIR)
            sp.wait_ge(abs_ready, 2 * NPAIR)
            sp.dma_start(DL[:].rearrange("p h f n -> p (h f n)")[:, 0:2 * C], wcls).then_inc(cls_loaded, 16)
            for pair in range(0, PAIRS, 2):
                store(FIRST + pair, XA, stored_xa)
                if pair + 2 < PAIRS:
                    reload_xa(pair + 2)
                else:
                    for h in range(2):
                        sp.wait_ge(stored_xa[h], 8 * pair + 32)
                    sp.dma_start(XA[:].rearrange("p k n -> p (k n)")[:, 0:KC * B * T], xcls).then_inc(cls_loaded, 16)
                store(FIRST + pair + 1)
                if pair + 2 < PAIRS:
                    load_xc(FIRST + pair + 3, FIRST + pair // 2 + 1)
            sp.wait_ge(cls_out, KC)
            sp.dma_start(outcls, XA[:].rearrange("p k n -> p (k n)")[:, 0:KC * B * T]).then_inc(cls_stored, 16)
            for h in range(2):
                sp.wait_ge(stored[h], 16 * (FIRST + PAIRS // 2) + 16)
            sp.wait_ge(cls_stored, 16)

        @block.tensor
        def _(pe):
            setup = XC[0:HA].rearrange("p k n -> p (k n)")
            TPW = setup[:, 0:2 * A].rearrange("p (h c) -> p h c", h=2)
            W1T = setup[:, 2 * A:NSETUP].rearrange("p (h n) -> p h n", h=2)
            pe.wait_ge(wts_loaded, 16 * (WEIGHT_LOADS - 1))
            pe.wait_ge(consts_set, 4)
            for m in range(2):
                for h in range(2):
                    mm = nc.tensor.matmul(PS[0:HA, m, 0:HID], TPW[:, h, HA * m:HA * m + HA], W1T[:, h, :],
                                          start=(h == 0), stop=(h == 1))
                mm.then_inc(setup_pe, 1)
            b2 = vec("mlp_b2")
            for h in range(2):
                mm = nc.tensor.matmul(PS[0:HA, 2, 0:1], ONES[:, 0:HA], b2[:, h:h + 1], start=(h == 0), stop=(h == 1))
            mm.then_inc(setup_pe, 1)
            pe.sem_inc(xa_used, 2)
            for done in (w1_done, w2_done, stats_done):
                pe.sem_inc(done, 1)
            pe.wait_ge(setup_act, 1)
            pe.wait_ge(setup_dve, 7)

            def down_start(s):
                pe.wait_ge(h_ready, KH * s)

            def down_blocks(s, blocks):
                for k in blocks:
                    if k % HK == 0:
                        pe.wait_ge(xa_loaded[k // HK], 16 * s + 16)
                    for m in range(2):
                        mm = nc.tensor.matmul(PS[0:HA, m, 0:PT], WD[:, k, HA * m:HA * m + HA], XA[:, k, :],
                                              start=(k == 0), stop=(k == KC - 1))
                    if k % HK == HK - 1:
                        mm.then_inc(xa_used, 1)

            def down(s):
                down_start(s)
                down_blocks(s, range(KC))

            def local(s):
                pe.wait_ge(conv_gelu, 2 * s + 2)
                pe.wait_ge(trans_out, 2 * s + 1)
                for m in range(2):
                    for h in range(2):
                        mm = nc.tensor.matmul(PS[0:HA, 2 + m, 0:PT], LPW[:, h, HA * m:HA * m + HA], GL[:, h, :],
                                              start=(h == 0), stop=(h == 1))
                mm.then_inc(lpw_done, 1)

            def salience(s):
                pe.wait_ge(abs_summed, s + 1)
                pe.wait_ge(newton_a, s)
                nc.tensor.matmul(PS[0:1, 7, 0:PT], ONES[:, 0:1], ADS[:], start=True, stop=True).then_inc(sal_ready, 1)

            def hidden(s, blocks=range(KH), with_a=True):
                if blocks[0] == 0:
                    pe.wait_ge(tconv_gelu, s + 1)
                    if with_a:
                        pe.wait_ge(ph_ready, 2 * s + 4)
                    pe.wait_ge(newton_a, s + 1)
                for m in blocks:
                    for h in range(2):
                        mm = nc.tensor.matmul(PS[:, (0, 1, 6)[m], 0:PT], W1P[:, h, 128 * m:128 * m + 128], TV[:, h, :],
                                              start=(h == 0), stop=(h == 1))
                    mm.then_inc(w1_done, 1)

            def transition(s, blocks=range(KH)):
                if blocks[0] == 0:
                    pe.wait_ge(local_out, s + 1)
                for k in blocks:
                    pe.wait_ge(h_ready, KH * s + (KH + k + 1))
                    for m in range(2):
                        mm = nc.tensor.matmul(PS[0:HA, 2 + m, 0:PT], W2[:, k, HA * m:HA * m + HA], H1[:, k, :],
                                              start=(k == 0), stop=(k == KH - 1))
                if blocks[-1] == KH - 1:
                    mm.then_inc(w2_done, 1)

            def stats(s, with_a=True):
                for n in range(2):
                    pe.wait_ge(sq_summed, 2 * s + (n + 2))
                    if n and with_a:
                        pe.wait_ge(topk_step, 5 * s + 10)
                    mm = nc.tensor.matmul(PS[0:HA, 6 + n, 0:PT], ONES[:, 0:HA], SQS[:, n, :], start=True, stop=True)
                mm.then_inc(stats_done, 1)

            def up_block(k, m, bank=4):
                pe.wait_ge(resid, KC * k + (m + 1))
                for h in range(2):
                    mm = nc.tensor.matmul(PS[:, bank + m % 2, 0:PT], UP[:, h, 128 * m:128 * m + 128],
                                          FU[:, k & 1, h, :], start=(h == 0), stop=(h == 1))
                mm.then_inc(up_done, 1)

            def up(k):
                pe.wait_ge(scattered, k + 2)
                for m in range(KC):
                    up_block(k, m)

            def up_in_chain(k, m):
                if m == 0:
                    pe.wait_ge(scattered, k + 2)
                    pe.wait_ge(trans_out, 2 * k + (2 * PAIRS + 3))
                up_block(k, m, 2)

            def heads(c):
                if not isinstance(c, int) or c:
                    pe.wait_ge(resid, KC * PAIRS * c - (KC - 2))
                pe.wait_ge(chain_dve, after("dve", c, "tok"))
                for part in range(2):
                    for hd in range(HEADS):
                        col = part * A + hd * DH
                        for h in range(2):
                            mm = nc.tensor.matmul(PS[0:DH, 4 + part, hd * NANC:(hd + 1) * NANC], AIN[:, h, col:col + DH],
                                                  TOK[:, h, :], start=(h == 0), stop=(h == 1))
                mm.then_inc(chain_pe, 1)

            def values(c):
                pe.wait_ge(chain_dve, after("dve", c, "q"))
                for h in range(2):
                    mm = nc.tensor.matmul(PS[:, 4, 0:A], TOK[:, h, :], AIN[:, h, 2 * A:3 * A], start=(h == 0), stop=(h == 1))
                mm.then_inc(chain_pe, 1)

            def scores(c):
                pe.wait_ge(chain_dve, after("dve", c, "k"))
                for hd in range(HEADS):
                    mm = nc.tensor.matmul(PS[:, 5, hd * NANC:(hd + 1) * NANC], QH[:, hd, :], KHD[:, hd, :], start=True, stop=True)
                mm.then_inc(chain_pe, 1)

            def turn(c):
                pe.wait_ge(chain_act, after("act", c, "v"))
                pe.wait_ge(chain_dve, after("dve", c, "prob"))
                for hd in range(HEADS):
                    mm = nc.tensor.transpose(PS[:, 4, hd * NANC:(hd + 1) * NANC], S[:, hd, :], IDENT)
                mm.then_inc(chain_pe, 1)

            def mix(c):
                pe.wait_ge(chain_dve, after("dve", c, "turned"))
                for hd in range(HEADS):
                    mm = nc.tensor.matmul(PS[0:DH, 5, hd * NANC:(hd + 1) * NANC], VV[:, hd * DH:(hd + 1) * DH], ST[:, hd, :],
                                          start=True, stop=True)
                mm.then_inc(chain_pe, 1)

            def attn_out(c):
                pe.wait_ge(chain_dve, after("dve", c, "mixed"))
                for m in range(2):
                    for hd in range(HEADS):
                        mm = nc.tensor.matmul(PS[0:HA, 4, m * NANC:(m + 1) * NANC], AOUT[:, hd, HA * m:HA * m + HA],
                                              OH[:, hd, :], start=(hd == 0), stop=(hd == HEADS - 1))
                mm.then_inc(chain_pe, 1)

            def anchors(c):
                pe.wait_ge(chain_dve, after("dve", c, "out"))
                for m in range(2):
                    for h in range(2):
                        mm = nc.tensor.matmul(PS[0:HA, 5, m * NANC:(m + 1) * NANC], APR[:, h, HA * m:HA * m + HA],
                                              A1[:, h, :], start=(h == 0), stop=(h == 1))
                mm.then_inc(chain_pe, 1)

            def mean_gate1(c):
                pe.wait_ge(chain_dve, after("dve", c, "ap_scaled"))
                for h in range(2):
                    nc.tensor.matmul(PS[0:HA, 4, 0:NANC], ONES[:, 0:HA], A2[:, h, :], start=(h == 0), stop=(h == 1))
                for m in range(2):
                    for q in range(4):
                        mm = nc.tensor.matmul(PS[0:HA, 4, 256 + m:257 + m], GW1[:, q, HA * m:HA * m + HA],
                                              GIN[:, q:q + 1], start=(q == 0), stop=(q == 3))
                mm.then_inc(chain_pe, 1)

            def anchor_var(c):
                pe.wait_ge(chain_act, after("act", c, "square"))
                for h in range(2):
                    mm = nc.tensor.matmul(PS[0:HA, 5, 0:NANC], ONES[:, 0:HA], ASQ[:, h, :], start=(h == 0), stop=(h == 1))
                mm.then_inc(chain_pe, 1)

            def gate2(c):
                pe.wait_ge(chain_act, after("act", c, "gelu"))
                for q in range(6):
                    for h in range(2):
                        mm = nc.tensor.matmul(PS[0:HA, 4, 300 + q:301 + q], GW2[:, h, HA * q:HA * q + HA], GH[:, h:h + 1],
                                              start=(h == 0), stop=(h == 1))
                mm.then_inc(chain_pe, 1)

            def after_down(s):
                local(s - 1)
                hidden(s - 1, (0,))
                salience(s)
                hidden(s - 1, (1, 2))
                transition(s - 1)

            def chain_end(c, with_up=True):
                k = c * PAIRS - 1
                ups = (lambda blocks: [up_in_chain(k, m) for m in blocks]) if with_up else (lambda blocks: None)
                anchors(c)
                ups((0,))
                mean_gate1(c)
                ups((1,))
                gate2(c)
                anchor_var(c)
                ups((2, 3, 4, 5))

            def first_pair(b, with_up=True):
                s, c = b * PAIRS, b - 1
                down_start(s)
                down_blocks(s, (0, 1, 2, 3))
                stats(s - 2)
                heads(c)
                down_blocks(s, (4, 5))
                values(c)
                scores(c)
                local(s - 1)
                hidden(s - 1, (0, 1))
                salience(s)
                hidden(s - 1, (2,))
                turn(c)
                transition(s - 1, (0,))
                mix(c)
                transition(s - 1, (1,))
                attn_out(c)
                transition(s - 1, (2,))
                chain_end(c, with_up)

            def other_pairs(b):
                with pe.Fori(1, PAIRS) as j:
                    s = b * PAIRS + j
                    k = s - (PAIRS + 1)
                    down_start(s)
                    down_blocks(s, (0, 1, 2))
                    pe.wait_ge(scattered, k + 2)
                    up_block(k, 0)
                    down_blocks(s, (3,))
                    up_block(k, 1)
                    stats(s - 2)
                    down_blocks(s, (4,))
                    up_block(k, 2)
                    down_blocks(s, (5,))
                    for m in (3, 4, 5):
                        up_block(k, m)
                    after_down(s)

            down(0)
            salience(0)
            down(1)
            after_down(1)
            with pe.Fori(2, PAIRS) as j:
                down_start(j)
                down_blocks(j, (0, 1, 2))
                stats(j - 2)
                down_blocks(j, (3, 4, 5))
                after_down(j)
            first_pair(1, False)
            with pe.Fori(2, B) as b:
                other_pairs(b - 1)
                first_pair(b)
            other_pairs(B - 1)
            s, c = NPAIR, B - 1
            heads(c)
            values(c)
            scores(c)
            stats(s - 2, False)
            turn(c)
            mix(c)
            attn_out(c)
            anchors(c)
            mean_gate1(c)
            gate2(c)
            anchor_var(c)
            local(s - 1)
            hidden(s - 1, (0, 1, 2), False)
            pe.wait_ge(scattered, s - PAIRS + 1)
            for m, step in ((0, "gate2"), (1, "newton1")):
                pe.wait_ge(chain_dve, after("dve", c, step))
                up_block(s - PAIRS - 1, m)
            transition(s - 1)
            for m in range(2, KC):
                up_block(s - PAIRS - 1, m)
            stats(s - 1, False)
            with pe.Fori(NPAIR - PAIRS, NPAIR) as k:
                up(k)
            pe.wait_ge(cls_loaded, 32)
            pe.wait_ge(cls_mean, 1)
            WC = DL[:].rearrange("p h f n -> p (h f n)")[:, 0:2 * C].rearrange("p (h n) -> p h n", h=2)
            for m in range(KC):
                pe.wait_ge(resid, KC * NPAIR + 2)
                if m >= 2:
                    pe.wait_ge(cls_out, m - 1)
                for h in range(2):
                    mm = nc.tensor.matmul(PS[:, 4 + m % 2, 0:B * T], WC[:, h, 128 * m:128 * m + 128], FS[:, h, :],
                                          start=(h == 0), stop=(h == 1))
                mm.then_inc(cls_mm, 1)

        @block.scalar
        def _(act):
            act.sem_inc(h_ready, KH)
            act.sem_inc(trans_out, 1)
            act.wait_ge(setup_pe, 2)
            act.wait_ge(consts_set, 4)
            nc.scalar.activation(W1P[:], PS[0:HA, 0:2, 0:HID], ACT.Identity).then_inc(setup_act, 1)
            act.wait_ge(setup_dve, 7)

            def take_ph(s, j):
                act.wait_ge(xa_used, 2 * s + 4)
                hold(act, delta_ready, 2 * s)
                for h in range(2):
                    nc.scalar.activation(window(PH, h, ph_base(j & 1)),
                                         PS[0:HA, h, 0:PT].rearrange("p (f r c) -> p f r c", f=2, c=SIDE),
                                         ACT.Identity, bias=vec("down_b")[:, h:h + 1]).then_inc(ph_ready, 1)

            def take_abs(s, b, j):
                act.wait_ge(delta_ready, 2 * s + 2)
                hold(act, abs_summed, s)
                for h in range(2):
                    nc.scalar.activation(AD[:, h, :], DL[:, h, ds(2 * j + 1, 2), :].rearrange("p f n -> p (f n)"), ACT.Abs,
                                         accum_out=DPS[:, h, b & 1, ds(j, 1)]).then_inc(abs_ready, 1)

            def take_local(s, j):
                act.wait_ge(lpw_done, s + 1)
                hold(act, fused, s + 1)
                nc.scalar.activation(NRM[:, 0:2, j, :], halves(2), ACT.Identity).then_inc(local_out, 1)

            def square_local(s, j):
                act.wait_ge(local_out, s + 1)
                hold(act, sq_summed, 2 * s + 1)
                nc.scalar.activation(SQ[:], NRM[:, 0:2, j, :], ACT.Square).then_inc(sq_ready, 1)

            def tconv_gelu_of(s):
                act.wait_ge(tconv_taps, 6 * s + 6)
                nc.scalar.activation(TV[:], TV[:], ACT.Gelu).then_inc(tconv_gelu, 1)

            def hidden_gelus(s):
                act.wait_ge(w2_done, s + 1)
                for m in range(KH):
                    act.wait_ge(w1_done, KH * s + (m + 2))
                    nc.scalar.activation(H1[:, m, :], PS[:, (0, 1, 6)[m], 0:PT], ACT.Gelu,
                                         bias=VP[:, m:m + 1]).then_inc(h_ready, 1)

            def take_transition(s, j):
                hold(act, w2_done, s + 2)
                for h in range(2):
                    nc.scalar.activation(NRM[:, 2 + h, j, :], PS[0:HA, 2 + h, 0:PT], ACT.Identity,
                                         bias=vec("mlp_b2")[:, h:h + 1]).then_inc(trans_out, 1)
                act.wait_ge(trans_out, 2 * s + 3)
                hold(act, sq_summed, 2 * s + 2)
                nc.scalar.activation(SQ[:], NRM[:, 2:4, j, :], ACT.Square).then_inc(sq_ready, 1)

            def conv_gelus(s):
                act.wait_ge(conv_taps, 18 * s + 18)
                act.wait_ge(lpw_done, s)
                for h in range(2):
                    nc.scalar.activation(GL[:, h, :].rearrange("p (f r c) -> p f r c", f=2, c=SIDE),
                                         window(CV, h, 0), ACT.Gelu).then_inc(conv_gelu, 1)

            def gelu_table():
                nc.scalar.activation(WARM[:], EPSC[:], ACT.Gelu)

            def rsqrts(s):
                act.wait_ge(stats_done, s + 2)
                act.wait_ge(normed, s + 1)
                act.wait_ge(normed_trans, s + 1)
                nc.scalar.activation(RY[:], halves(6), ACT.Abs_reciprocal_sqrt, bias=EPSC[:]).then_inc(rs_first, 1)
                act.wait_ge(rs_first, s + 1)
                nc.scalar.activation(RT[:], RY[:], ACT.Square).then_inc(rs_square, 1)

            def weigh(k, j):
                hold(act, fused, k + PAIRS)
                for h in range(2):
                    nc.scalar.activation(FT[:, h, :], NRM[:, 2 + h, j, :], ACT.Identity, bias=GC[:, h:h + 1],
                                         scale=GG[:, 2 + h:3 + h]).then_inc(weighted, 1)

            def take_values(c):
                act.wait_ge(chain_pe, after("pe", c, "v"))
                nc.scalar.activation(VV[:], PS[:, 4, 0:A], ACT.Identity).then_inc(chain_act, 1)

            def attn_exp(c):
                act.wait_ge(chain_dve, after("dve", c, "shifted"))
                nc.scalar.activation(S[:], S[:], ACT.Exp).then_inc(chain_act, 1)

            def anchor_squares(c):
                act.wait_ge(chain_dve, after("dve", c, "centred"))
                nc.scalar.activation(ASQ[:], XCN[:], ACT.Square).then_inc(chain_act, 1)

            def gate_gelu(c):
                act.wait_ge(chain_dve, after("dve", c, "gate1"))
                nc.scalar.activation(GH[:], GH[:], ACT.Gelu).then_inc(chain_act, 1)

            def gate_exp(c):
                act.wait_ge(chain_dve, after("dve", c, "gshift"))
                nc.scalar.activation(GT[:], GT[:], ACT.Exp).then_inc(chain_act, 1)

            def anchor_rsqrt(c):
                act.wait_ge(chain_pe, after("pe", c, "var"))
                nc.scalar.activation(AY[:], PS[0:HA, 5, 0:NANC], ACT.Abs_reciprocal_sqrt, bias=EPSC[:]).then_inc(chain_act, 1)
                act.wait_ge(chain_act, after("act", c, "rsqrt"))
                nc.scalar.activation(AT[:], AY[:], ACT.Square).then_inc(chain_act, 1)

            def first_pair(b):
                s, c = b * PAIRS, b - 1
                rsqrts(s - 2)
                gelu_table()
                take_ph(s, 0)
                conv_gelus(s - 1)
                take_values(c)
                tconv_gelu_of(s - 1)
                take_abs(s, b, 0)
                attn_exp(c)
                take_local(s - 1, PAIRS - 1)
                hidden_gelus(s - 1)
                square_local(s - 1, PAIRS - 1)
                take_transition(s - 1, PAIRS - 1)
                anchor_squares(c)
                gate_gelu(c)
                gate_exp(c)
                anchor_rsqrt(c)
                act.wait_ge(chain_dve, after("dve", c, "const2"))
                weigh(s - PAIRS, 0)

            def pair(s, b, j, with_conv=True):
                take_ph(s, j)
                if with_conv:
                    conv_gelus(s - 1)
                tconv_gelu_of(s - 1)
                take_abs(s, b, j)
                take_local(s - 1, j - 1)
                square_local(s - 1, j - 1)
                hidden_gelus(s - 1)
                take_transition(s - 1, j - 1)

            def other_pairs(b):
                with act.Fori(1, PAIRS) as j:
                    s = b * PAIRS + j
                    weigh(s - PAIRS, j)
                    rsqrts(s - 2)
                    gelu_table()
                    pair(s, b, j)

            take_ph(0, 0)
            take_abs(0, 0, 0)
            pair(1, 0, 1)
            with act.Fori(2, PAIRS) as j:
                conv_gelus(j - 1)
                rsqrts(j - 2)
                gelu_table()
                pair(j, 0, j, False)
            first_pair(1)
            with act.Fori(2, B) as b:
                other_pairs(b - 1)
                first_pair(b)
            other_pairs(B - 1)
            s, c = NPAIR, B - 1
            take_values(c)
            attn_exp(c)
            rsqrts(s - 2)
            anchor_squares(c)
            gate_gelu(c)
            conv_gelus(s - 1)
            tconv_gelu_of(s - 1)
            gate_exp(c)
            anchor_rsqrt(c)
            act.wait_ge(chain_dve, after("dve", c, "const2"))
            weigh(NPAIR - PAIRS, 0)
            take_local(s - 1, PAIRS - 1)
            square_local(s - 1, PAIRS - 1)
            hidden_gelus(s - 1)
            take_transition(s - 1, PAIRS - 1)
            weigh(NPAIR - PAIRS + 1, 1)
            rsqrts(s - 1)
            with act.Fori(2, PAIRS) as j:
                weigh(NPAIR - PAIRS + j, j)

        @block.gpsimd
        def _(pool):
            pool.memset(PH[:], 0.0).then_inc(consts_set, 1)
            pool.memset(DL[:, :, 0, :], 0.0).then_inc(consts_set, 1)
            pool.memset(DL[:, :, T + 1, :], 0.0).then_inc(consts_set, 1)
            for done in (gathered, sq_summed, scattered, normed_trans):
                pool.sem_inc(done, 1)
            pool.wait_ge(consts_set, 4)

            def sum_abs(s):
                pool.wait_ge(abs_ready, 2 * s + 2)
                pool.wait_ge(sal_ready, s)
                nc.gpsimd.tensor_tensor(ADS[:], AD[:, 0, :], AD[:, 1, :], ALU.add).then_inc(abs_summed, 1)

            def sum_squares(s, n):
                pool.wait_ge(sq_ready, 2 * s + (n + 1))
                pool.wait_ge(stats_done, s + 1)
                nc.gpsimd.tensor_tensor(SQS[:, n, :], SQ[:, 0, :], SQ[:, 1, :], ALU.add).then_inc(sq_summed, 1)

            def tokens(k):
                for f in range(2):
                    yield f, nc.values_load_multi_w_load_instructions(
                        IDX[0:1, k & (2 * PAIRS - 1), f * TOPK:(f + 1) * TOPK], engines=[pool.engine],
                        min_val=0, max_val=HW - 1)[1]

            def gather(s, b, j):
                pool.wait_ge(topk_step, 5 * s + 5)
                for f, frame in tokens(s):
                    for r, token in enumerate(frame):
                        last = nc.gpsimd.tensor_copy(G[:, b & 1, :, ds((2 * j + f) * TOPK + r, 1)],
                                                     PD[:, s & 1, :, ds(token + f * HW, 1)])
                last.then_inc(gathered, 1)

            def scatter(k, j):
                for f, frame in tokens(k):
                    if f == 0:
                        hold(pool, fused, k + (PAIRS + 1))
                    for r, token in enumerate(frame):
                        at = FU[:, k & 1, :, ds(token + f * HW, 1)]
                        last = nc.gpsimd.tensor_tensor(at, at, Z[:, :, ds((2 * j + f) * TOPK + r, 1)], ALU.add)
                last.then_inc(scattered, 1)

            def norm_transition(s, j):
                hold(pool, newton_c, s + 1)
                at = NRM[:, 2:4, j, :]
                nc.gpsimd.tensor_tensor(at, at, RY[:, 1:2, :].to_broadcast([HA, 2, PT]), ALU.mult).then_inc(normed_trans, 1)

            def first_pair(b):
                s = b * PAIRS
                sum_abs(s)
                sum_squares(s - 1, 0)
                norm_transition(s - 2, PAIRS - 2)
                gather(s, b, 0)
                sum_squares(s - 1, 1)
                scatter(s - PAIRS, 0)

            def other_pairs(b):
                with pool.Fori(1, PAIRS) as j:
                    s = b * PAIRS + j
                    scatter(s - PAIRS, j)
                    sum_abs(s)
                    sum_squares(s - 1, 0)
                    norm_transition(s - 2, (j + (PAIRS - 2)) & (PAIRS - 1))
                    gather(s, b, j)
                    sum_squares(s - 1, 1)

            sum_abs(0)
            gather(0, 0, 0)
            sum_abs(1)
            sum_squares(0, 0)
            gather(1, 0, 1)
            sum_squares(0, 1)
            with pool.Fori(2, PAIRS) as j:
                sum_abs(j)
                sum_squares(j - 1, 0)
                norm_transition(j - 2, j - 2)
                sum_squares(j - 1, 1)
                gather(j, 0, j)
            first_pair(1)
            with pool.Fori(2, B) as b:
                other_pairs(b - 1)
                first_pair(b)
            other_pairs(B - 1)
            scatter(NPAIR - PAIRS, 0)
            sum_squares(NPAIR - 1, 0)
            norm_transition(NPAIR - 2, PAIRS - 2)
            sum_squares(NPAIR - 1, 1)
            scatter(NPAIR - PAIRS + 1, 1)
            norm_transition(NPAIR - 1, PAIRS - 1)
            with pool.Fori(2, PAIRS) as j:
                scatter(NPAIR - PAIRS + j, j)

        @block.vector
        def _(dve):
            v = nc.vector
            dve.sem_inc(newton_a, 1)
            dve.sem_inc(normed, 1)
            dve.sem_inc(fused, PAIRS)
            dve.sem_inc(resid, 2)
            dve.sem_inc(frames_summed, 2)
            dve.sem_inc(up_done, 2 * KC)
            v.memset(EPSC[:], EPS)
            v.memset(ONES[:], 1.0 / A).then_inc(consts_set, 1)
            dve.wait_ge(consts_set, 4)
            dve.wait_ge(wts_loaded, 16 * (WEIGHT_LOADS - 1))
            v.tensor_reduce(WM[0:HA, 0:2], LPW, AX.X, ALU.add)
            v.tensor_reduce(WM[:, 2:2 + KH], W2[:], AX.X, ALU.add).then_inc(setup_dve, 1)
            dve.wait_ge(setup_dve, 1)
            v.tensor_scalar(WM[:, 2:2 + KH], WM[:, 2:2 + KH], 1.0 / A, None, ALU.mult).then_inc(setup_dve, 1)
            v.tensor_scalar(WM[0:HA, 0:2], WM[0:HA, 0:2], 1.0 / A, None, ALU.mult).then_inc(setup_dve, 1)
            dve.wait_ge(setup_dve, 3)
            for h in range(2):
                v.tensor_scalar(LPW[:, h, :], LPW[:, h, :], WM[0:HA, h:h + 1], None, ALU.subtract)
            for k in range(KH):
                v.tensor_scalar(W2[:, k, :], W2[:, k, :], WM[:, 2 + k:3 + k], None, ALU.subtract).then_inc(setup_dve, 1)
            dve.wait_ge(setup_pe, 3)
            v.tensor_tensor(vec("mlp_b2"), vec("mlp_b2"), PS[0:HA, 2, 0:1].to_broadcast([HA, 2]), ALU.subtract).then_inc(setup_dve, 1)

            def delta(s, b, j):
                dve.wait_ge(ph_ready, 2 * s + 2)
                here = ph_base(j & 1)
                before = here if isinstance(j, int) and j == 0 else ph_base(1 - (j & 1)) + FP
                for f, prev in ((0, before), (1, here)):
                    v.tensor_tensor(DL[:, :, ds(2 * j + 1 + f, 1), :].rearrange("p h f (r c) -> p h (f r) c", c=SIDE),
                                    frame2(PH, here + f * FP), frame2(PH, prev), ALU.subtract).then_inc(delta_ready, 1)

            def anchor_source(s, j):
                dve.wait_ge(gathered, s)
                for f in range(2):
                    dve.wait_ge(delta_ready, 2 * s + (f + 1))
                    v.tensor_tensor(PD[:, s & 1, :, f * HW:(f + 1) * HW].rearrange("p h (r c) -> p h r c", c=SIDE),
                                    frame2(PH, ph_base(j & 1) + f * FP),
                                    DL[:, :, ds(2 * j + 1 + f, 1), :].rearrange("p h f (r c) -> p h (f r) c", c=SIDE),
                                    ALU.add).then_inc(ph_delta, 1)

            def tconv(s, j, taps, with_a=True):
                for k in taps:
                    if k == 0:
                        dve.wait_ge(w1_done, KH * s + 1)
                        dve.wait_ge(delta_ready, 2 * s + 2)
                    if k == 2 and with_a:
                        dve.wait_ge(delta_ready, 2 * s + 3)
                    for h in range(2):
                        src = DL[:, h, ds(2 * j + k, 2), :].rearrange("p f n -> p (f n)")
                        if k == 0:
                            tap = v.tensor_scalar(TV[:, h, :], src, TDW[:, h, 0:1], None, ALU.mult)
                        else:
                            dve.wait_ge(tconv_taps, 6 * s + (2 * k + h - 1))
                            tap = v.scalar_tensor_tensor(out=TV[:, h, :], in0=src, scalar=TDW[:, h, k:k + 1],
                                                         in1=TV[:, h, :], op0=ALU.mult, op1=ALU.add)
                        tap.then_inc(tconv_taps, 1)

            def conv_taps_of(s, j, first, last):
                for step in range(first, last):
                    k, h = step // 2, step % 2
                    src = rows(PH, h, ph_base(j & 1) + (k // 3 - 1) * PITCH + (k % 3 - 1))
                    dst = rows(CV, h, 0)
                    if k == 0:
                        if h == 0:
                            dve.wait_ge(conv_gelu, 2 * s)
                        tap = v.tensor_scalar(dst, src, LDW[:, h, 0:1], None, ALU.mult)
                    else:
                        dve.wait_ge(conv_taps, 18 * s + (step - 1))
                        tap = v.scalar_tensor_tensor(out=dst, in0=src, scalar=LDW[:, h, k:k + 1], in1=dst,
                                                     op0=ALU.mult, op1=ALU.add)
                    tap.then_inc(conv_taps, 1)

            def frame_sums(k):
                dve.wait_ge(scattered, k + 2)
                v.tensor_reduce(FS[:, :, ds(2 * k, 2)], FU[:, k & 1, :, :].rearrange("p h (f n) -> p h f n", f=2), AX.X, ALU.add).then_inc(frames_summed, 1)

            def residual(k, m, bank=4, place=XC, signal=xc_loaded, loads=None):
                loads = k + 1 if loads is None else loads
                dve.wait_ge(up_done, KC * k + (m + 1 + 2 * KC))
                if m % HK == 0:
                    dve.wait_ge(signal[m // HK], 16 * loads)
                v.scalar_tensor_tensor(out=place[:, m, :], in0=PS[:, bank + m % 2, 0:PT], scalar=VP[:, KH + m:KH + m + 1],
                                       in1=place[:, m, :], op0=ALU.add, op1=ALU.add).then_inc(resid, 1)

            def topk(s):
                hold(dve, sal_ready, s + 1)
                for f in range(2):
                    sal = PS[0:1, 7, f * HW:(f + 1) * HW]
                    v.max(MX[:, f, :], sal).then_inc(topk_step, 1)
                for f in range(2):
                    sal = PS[0:1, 7, f * HW:(f + 1) * HW]
                    hold(dve, topk_step, 5 * s + 2)
                    v.max_index(IDN[:, f * TOPK:(f + 1) * TOPK], MX[:, f, :], sal).then_inc(topk_step, 1)
                dve.wait_ge(topk_step, 5 * s + 4)
                v.tensor_copy(IDX[0:1, s & (2 * PAIRS - 1), :], IDN[:]).then_inc(topk_step, 1)

            def fuse(k, j):
                dve.wait_ge(up_done, KC * k + KC)
                dve.wait_ge(frames_summed, k + 1)
                for h in range(2):
                    dve.wait_ge(weighted, 2 * k + (h + 1))
                    last = v.scalar_tensor_tensor(out=FU[:, k & 1, h, :], in0=NRM[:, h, j, :], scalar=GG[:, h:h + 1],
                                                  in1=FT[:, h, :], op0=ALU.mult, op1=ALU.add)
                last.then_inc(fused, 1)

            def newton_start(s):
                dve.wait_ge(rs_square, s + 1)
                v.scalar_tensor_tensor(out=RT[:], in0=halves(6), scalar=EPSC[:], in1=RT[:],
                                       op0=ALU.add, op1=ALU.mult).then_inc(newton_a, 1)

            def newton_end(s, j):
                dve.wait_ge(newton_a, s + 2)
                v.tensor_scalar(RT[:], RT[:], -0.5, 1.5, ALU.mult, ALU.add).then_inc(newton_b, 1)
                dve.wait_ge(newton_b, s + 1)
                v.tensor_tensor(RY[:], RY[:], RT[:], ALU.mult).then_inc(newton_c, 1)
                dve.wait_ge(newton_c, s + 1)
                at = NRM[:, 0:2, j, :]
                v.tensor_tensor(at, at, RY[:, 0:1, :].to_broadcast([HA, 2, PT]), ALU.mult).then_inc(normed, 1)

            def link(instruction, c, step):
                instruction.then_inc(chain_dve, 1)
                dve.wait_ge(chain_dve, after("dve", c, step))

            def clip_delta(c):
                link(v.tensor_reduce(GIN[:, 0:2], DPS[:, :, c & 1, :], AX.X, ALU.add), c, "dp")
                link(v.tensor_scalar(GIN[:, 0:2], GIN[:, 0:2], 1.0 / (T * HW), None, ALU.mult), c, "dp_scaled")
                dve.wait_ge(gathered, PAIRS * c + (PAIRS + 1))
                link(v.tensor_copy(TOK[:], G[:, c & 1, :, :]), c, "tok")

            def take_heads(c):
                dve.wait_ge(chain_pe, after("pe", c, "qk"))
                for part, dst, step in ((0, QH, "q"), (1, KHD, "k")):
                    link(v.tensor_tensor(dst[:], PS[0:DH, 4 + part, 0:HEADS * NANC].rearrange("p (h n) -> p h n", h=HEADS),
                                         VH[:, part, :].unsqueeze(2).to_broadcast([DH, HEADS, NANC]), ALU.add), c, step)

            def softmax_top(c):
                dve.wait_ge(chain_pe, after("pe", c, "scores"))
                link(v.scalar_tensor_tensor(out=S[:], in0=PS[:, 5, 0:HEADS * NANC].rearrange("p (h n) -> p h n", h=HEADS),
                                            scalar=float(DH) ** -0.5,
                                            in1=MASK.unsqueeze(1).to_broadcast([NANC, HEADS, NANC]),
                                            op0=ALU.mult, op1=ALU.add), c, "masked")
                link(v.tensor_reduce(SM[:, 0, :], S[:], AX.X, ALU.max), c, "max")
                link(v.tensor_tensor(S[:], S[:], SM[:, 0, :].unsqueeze(2).to_broadcast([NANC, HEADS, NANC]),
                                     ALU.subtract), c, "shifted")

            def softmax_end(c):
                dve.wait_ge(chain_act, after("act", c, "exp"))
                link(v.tensor_reduce(SM[:, 1, :], S[:], AX.X, ALU.add), c, "sum")
                link(v.reciprocal(SM[:, 2, :], SM[:, 1, :]), c, "recip")
                link(v.tensor_tensor(S[:], S[:], SM[:, 2, :].unsqueeze(2).to_broadcast([NANC, HEADS, NANC]),
                                     ALU.mult), c, "prob")

            def take_turned(c):
                dve.wait_ge(chain_pe, after("pe", c, "turned"))
                link(v.tensor_copy(ST[:], PS[:, 4, 0:HEADS * NANC].rearrange("p (h n) -> p h n", h=HEADS)), c, "turned")

            def take_mixed(c):
                dve.wait_ge(chain_pe, after("pe", c, "mixed"))
                link(v.tensor_tensor(OH[:], PS[0:DH, 5, 0:HEADS * NANC].rearrange("p (h n) -> p h n", h=HEADS),
                                     VH[:, 2, :].unsqueeze(2).to_broadcast([DH, HEADS, NANC]), ALU.add), c, "mixed")

            def take_projected(c, bank, dst, bias, step):
                dve.wait_ge(chain_pe, after("pe", c, step))
                link(v.tensor_tensor(dst[:], PS[0:HA, bank, 0:2 * NANC].rearrange("p (h n) -> p h n", h=2),
                                     vec(bias).unsqueeze(2).to_broadcast([HA, 2, NANC]), ALU.add), c, step)

            def take_anchors(c):
                take_projected(c, 5, A2, "proj_b", "anchor")
                link(v.tensor_reduce(GIN[:, 2:4], A2[:], AX.X, ALU.add), c, "ap")
                link(v.tensor_scalar(GIN[:, 2:4], GIN[:, 2:4], 1.0 / NANC, None, ALU.mult), c, "ap_scaled")

            def centre(c):
                dve.wait_ge(chain_pe, after("pe", c, "mean_gate1"))
                link(v.tensor_tensor(XCN[:], A2[:], PS[0:HA, 4, 0:NANC].unsqueeze(1).to_broadcast([HA, 2, NANC]),
                                     ALU.subtract), c, "centred")
                link(v.tensor_tensor(GH[:], vec("gate_b1"), PS[0:HA, 4, 256:258], ALU.add), c, "gate1")

            three = [HA, 3, 2]
            g3 = GT[:].rearrange("p (g h) -> p g h", h=2)

            def gates_top(c):
                dve.wait_ge(chain_pe, after("pe", c, "gate2"))
                link(v.tensor_tensor(GT[:], vec("gate_b2"), PS[0:HA, 4, 300:306], ALU.add), c, "gate2")
                link(v.tensor_tensor(GM[:], GT[:, 0:2], GT[:, 2:4], ALU.max), c, "gmax1")
                link(v.tensor_tensor(GM[:], GM[:], GT[:, 4:6], ALU.max), c, "gmax2")
                link(v.tensor_tensor(g3, g3, GM[:].unsqueeze(1).to_broadcast(three), ALU.subtract), c, "gshift")

            def gates_end(c):
                dve.wait_ge(chain_act, after("act", c, "gate_exp"))
                link(v.tensor_tensor(GM[:], GT[:, 0:2], GT[:, 2:4], ALU.add), c, "gsum1")
                link(v.tensor_tensor(GM[:], GM[:], GT[:, 4:6], ALU.add), c, "gsum2")
                link(v.reciprocal(GM[:], GM[:]), c, "grecip")
                link(v.tensor_tensor(g3, g3, GM[:].unsqueeze(1).to_broadcast(three), ALU.mult), c, "gates")
                link(v.tensor_tensor(GG[:], GT[:], vec("gain"), ALU.mult), c, "gains")
                link(v.tensor_tensor(GB[:], GT[:], vec("beta"), ALU.mult), c, "betas")
                link(v.tensor_tensor(GC[:], GB[:, 0:2], GB[:, 2:4], ALU.add), c, "const1")
                link(v.tensor_tensor(GC[:], GC[:], GB[:, 4:6], ALU.add), c, "const2")

            def anchor_norm(c):
                dve.wait_ge(chain_act, after("act", c, "rsqrt_sq"))
                link(v.scalar_tensor_tensor(out=AT[:], in0=PS[0:HA, 5, 0:NANC], scalar=EPSC[:], in1=AT[:],
                                            op0=ALU.add, op1=ALU.mult), c, "newton1")
                link(v.tensor_scalar(AT[:], AT[:], -0.5, 1.5, ALU.mult, ALU.add), c, "newton2")
                link(v.tensor_tensor(AY[:], AY[:], AT[:], ALU.mult), c, "newton3")
                dve.wait_ge(scattered, PAIRS * c + 1)
                link(v.tensor_tensor(Z[:], XCN[:], AY[:].unsqueeze(1).to_broadcast([HA, 2, NANC]), ALU.mult), c, "znorm")
                link(v.tensor_tensor(Z[:], Z[:], GG[:, 4:6].unsqueeze(2).to_broadcast([HA, 2, NANC]), ALU.mult), c, "z")

            def chain_end(c, with_up=True):
                def add(*blocks):
                    for m in blocks:
                        if with_up:
                            residual(c * PAIRS - 1, m, 2)

                take_projected(c, 4, A1, "out_b", "out")
                take_anchors(c)
                add(0)
                centre(c)
                add(1)
                gates_top(c)
                gates_end(c)
                add(2)
                anchor_norm(c)
                add(3)
                fuse(c * PAIRS, 0)
                add(4, 5)
                if with_up:
                    frame_sums(c * PAIRS - 1)

            def first_pair(b, with_up):
                s, c = b * PAIRS, b - 1
                conv_taps_of(s - 1, 1, 0 if with_up else 9, 11)
                clip_delta(c)
                conv_taps_of(s - 1, 1, 11, 18)
                tconv(s - 1, PAIRS - 1, (0, 1))
                take_heads(c)
                newton_start(s - 2)
                delta(s, b, 0)
                tconv(s - 1, PAIRS - 1, (2,))
                softmax_top(c)
                anchor_source(s, 0)
                softmax_end(c)
                take_turned(c)
                newton_end(s - 2, PAIRS - 2)
                take_mixed(c)
                topk(s)
                chain_end(c, with_up)

            def other_pairs(b):
                with dve.Fori(1, PAIRS) as j:
                    s = b * PAIRS + j
                    k = s - (PAIRS + 1)
                    conv_taps_of(s - 1, j - 1, 0, 14)
                    residual(k, 0)
                    fuse(s - PAIRS, j)
                    residual(k, 1)
                    conv_taps_of(s - 1, j - 1, 14, 18)
                    residual(k, 2)
                    newton_start(s - 2)
                    tconv(s - 1, j - 1, (0,))
                    residual(k, 3)
                    tconv(s - 1, j - 1, (1,))
                    delta(s, b, j)
                    tconv(s - 1, j - 1, (2,))
                    residual(k, 4)
                    residual(k, 5)
                    anchor_source(s, j)
                    frame_sums(k)
                    newton_end(s - 2, (j + (PAIRS - 2)) & (PAIRS - 1))
                    topk(s)

            delta(0, 0, 0)
            anchor_source(0, 0)
            topk(0)
            conv_taps_of(0, 0, 0, 18)
            tconv(0, 0, (0, 1))
            delta(1, 0, 1)
            tconv(0, 0, (2,))
            anchor_source(1, 1)
            conv_taps_of(1, 1, 0, 9)
            topk(1)
            with dve.Fori(2, PAIRS) as j:
                conv_taps_of(j - 1, j - 1, 9, 18)
                tconv(j - 1, j - 1, (0, 1))
                newton_start(j - 2)
                delta(j, 0, j)
                tconv(j - 1, j - 1, (2,))
                anchor_source(j, j)
                newton_end(j - 2, j - 2)
                conv_taps_of(j, j, 0, 9)
                topk(j)
            first_pair(1, False)
            with dve.Fori(2, B) as b:
                other_pairs(b - 1)
                first_pair(b, True)
            other_pairs(B - 1)
            s, c = NPAIR, B - 1
            clip_delta(c)
            take_heads(c)
            softmax_top(c)
            conv_taps_of(s - 1, 1, 0, 4)
            softmax_end(c)
            conv_taps_of(s - 1, 1, 4, 6)
            take_turned(c)
            conv_taps_of(s - 1, 1, 6, 8)
            take_mixed(c)
            conv_taps_of(s - 1, 1, 8, 14)
            take_projected(c, 4, A1, "out_b", "out")
            conv_taps_of(s - 1, 1, 14, 16)
            take_anchors(c)
            conv_taps_of(s - 1, 1, 16, 18)
            newton_start(s - 2)
            centre(c)
            tconv(s - 1, PAIRS - 1, (0, 1, 2), False)
            gates_top(c)
            gates_end(c)
            anchor_norm(c)
            fuse(NPAIR - PAIRS, 0)
            newton_end(s - 2, PAIRS - 2)
            for m in range(KC):
                residual(NPAIR - PAIRS - 1, m)
            frame_sums(NPAIR - PAIRS - 1)
            fuse(NPAIR - PAIRS + 1, 1)
            newton_start(s - 1)
            newton_end(s - 1, PAIRS - 1)
            for j in range(PAIRS):
                k = NPAIR - PAIRS + j
                if 0 < j < PAIRS - 1:
                    fuse(k + 1, j + 1)
                for m in range(KC):
                    if j % 2 == 0:
                        residual(k, m, 4, XA, xa_loaded, NPAIR + j // 2 + 1)
                    else:
                        residual(k, m, 4, XC, xc_loaded, NPAIR - PAIRS + j // 2 + 1)
                frame_sums(k)
            dve.wait_ge(frames_summed, NPAIR + 2)
            v.tensor_scalar(FS[:], FS[:], 1.0 / HW, None, ALU.mult).then_inc(cls_mean, 1)
            XK = XA[:].rearrange("p k n -> p (k n)")[:, 0:KC * B * T].rearrange("p (k n) -> p k n", k=KC)
            dve.wait_ge(cls_loaded, 32)
            for m in range(KC):
                dve.wait_ge(cls_mm, m + 1)
                v.scalar_tensor_tensor(out=XK[:, m, :], in0=PS[:, 4 + m % 2, 0:B * T],
                                       scalar=VP[:, KH + KC + m:KH + KC + m + 1], in1=XK[:, m, :],
                                       op0=ALU.add, op1=ALU.add).then_inc(cls_out, 1)


def kernel(**inputs):
    import numpy as np
    import concourse.bacc as bacc
    from concourse.bass_utils import run_bass_kernel_spmd

    a = {k.replace("L0_conv_", ""): np.asarray(v) for k, v in inputs.items()}
    x = a["x"]

    def by(n, w):
        k = w.shape[0] // n
        return w.reshape(k, n, *w.shape[1:]).swapaxes(0, 1)

    def flat(w):
        return w.reshape(w.shape[0], -1)

    vectors = {"down_b": by(HA, a["down_b"]), "mlp_b2": by(HA, a["tmlp_b2"]), "out_b": by(HA, a["attn_out_b"]),
               "gain": np.concatenate([by(HA, a[n]) for n in ("lnorm_g", "tnorm_g", "anorm_g")], 1),
               "beta": np.concatenate([by(HA, a[n]) for n in ("lnorm_b", "tnorm_b", "anorm_b")], 1),
               "proj_b": by(HA, a["aproj_b"]), "gate_b1": by(HA, a["gate_b1"]), "gate_b2": by(HA, a["gate_b2"]),
               "ldw": flat(by(HA, a["ldw_w"].reshape(A, 9))), "tdw": flat(by(HA, a["tdw_w"].reshape(A, 3)))}
    weights = {"lpw": a["lpw_w"], "up": a["up_w"], "attn_in": a["attn_in_w"], "aproj": a["aproj_w"],
               "gate1": a["gate_w1"], "gate2": a["gate_w2"]}
    place = np.arange(NANC)
    mask = np.where((place[:, None] - place[None, :]) % TOPK == 0, 0.0, -1e30)
    arrays = {
        "xp": x[:, :, 1:, :].reshape(B, PAIRS, 2, HW, KC, 128).transpose(0, 1, 5, 4, 2, 3).reshape(NPAIR, 128, KC, PT),
        "xcls": x[:, :, 0, :].reshape(B * T, KC, 128).transpose(2, 1, 0).reshape(128, KC * B * T),
        "wdown": by(128, a["down_w"].T),
        "w96": np.concatenate([flat(by(HA, weights[n].T)) for n in W96], 1),
        "wsetup": np.concatenate([flat(by(HA, a["tpw_w"])), flat(by(HA, a["tmlp_w1"].T))], 1),
        "wcls": flat(by(HA, a["cls_w"].T)),
        "w2": by(128, a["tmlp_w2"].T),
        "aout": by(DH, a["attn_out_w"].T),
        "v96": np.concatenate([vectors[n] for n in V96], 1),
        "v48": a["attn_in_b"].reshape(3, HEADS, DH).transpose(2, 0, 1),
        "v128": np.concatenate([by(128, a[n]) for n in ("tmlp_b1", "up_b", "cls_b")], 1),
        "consts": np.stack([np.eye(128), mask], 1).astype(np.float32),
    }
    arrays = {k: np.ascontiguousarray(v, dtype=np.float32) for k, v in arrays.items()}
    nc = bacc.Bacc("TRN2", target_bir_lowering=False, num_devices=1)
    args = [nc.dram_tensor(k, v.shape, F32, kind="ExternalInput").ap() for k, v in arrays.items()]
    args.append(nc.dram_tensor("out", (NPAIR, 128, KC, PT), F32, kind="ExternalOutput").ap())
    args.append(nc.dram_tensor("outcls", (128, KC * B * T), F32, kind="ExternalOutput").ap())
    build(nc, *args)
    r = run_bass_kernel_spmd(nc, [arrays], core_ids=[0]).results[0]
    patch = r["out"].reshape(B, PAIRS, 128, KC, 2, HW).transpose(0, 1, 4, 5, 3, 2).reshape(B, T, HW, C)
    cls = r["outcls"].reshape(128, KC, B * T).transpose(2, 1, 0).reshape(B, T, 1, C)
    return np.concatenate([cls, patch], 2)
```
